# Optimizing a Trainium2 kernel written in Bass

```python
import numpy as np
import jax
import jax.numpy as jnp

def _softmax(x, axis=-1):
    return jax.nn.softmax(x, axis=axis)

def _gelu(x):
    return jax.nn.gelu(x, approximate=True)

def _silu(x):
    return jax.nn.silu(x)

def _sigmoid(x):
    return jax.nn.sigmoid(x)

def _layernorm(x, axis=-1, eps=1e-05):
    m = jnp.mean(x, axis=axis, keepdims=True)
    v = jnp.var(x, axis=axis, keepdims=True)
    return (x - m) / jnp.sqrt(v + eps)

def _scatter_add(tgt, idx, src, axis=0):
    return tgt.at[idx].add(src)

def _segment_sum(src, seg, n):
    return jax.ops.segment_sum(src, seg, n)
kernel_name = 'mk_seq_preln_d1_jaxref_r8_6dc7f8'

def setup_inputs(seed: int=0):
    np.random.seed(seed)
    _w = jnp.asarray

    def _L0_attn_setup():
        import math
        import jax, jax.numpy as jnp
        import numpy as np
        B_SZ, L_SEQ, D_MODEL, N_STATE = (4, 512, 128, 16)
        DT_RANK = math.ceil(D_MODEL / 16)
        CONV_K = 3
        DT_MIN, DT_MAX = (0.001, 0.1)

        def _inverse_softplus(x):
            return x + jnp.log(1.0 - jnp.exp(-x))

        def _largest_factor_up_to(b, n):
            if n < 2:
                return n
            k = b
            while n % k != 0:
                k -= 1
            return k

        def _ssm_chunked_scan(x, A, Bc, Cc, dt):
            B, L, D = x.shape
            N = A.shape[-1]
            chunk = _largest_factor_up_to(int(math.sqrt(L)), L)
            nc = L // chunk
            r3 = lambda t, F: t.reshape(B, nc, chunk, F).transpose(1, 2, 0, 3)
            xc, dtc = (r3(x, D), r3(dt, D))
            bc, cc = (r3(Bc, N), r3(Cc, N))

            def assoc(lft, rgt):
                g_l, h_l = lft
                g_r, h_r = rgt
                return (g_l * g_r, g_r * h_l + h_r)

            def scan_chunk(carry, ch):
                g0, h0 = carry
                xk, bk, ck, dk = ch
                dA = jnp.exp(jnp.einsum('dn,lbd->lbdn', A, dk))
                dB = jnp.einsum('lbn,lbd,lbd->lbdn', bk, xk, dk)
                gs, hs = jax.lax.associative_scan(assoc, (dA, dB))
                hs = gs * h0 + hs
                yk = jnp.einsum('lbn,lbdn->lbd', ck, hs)
                return ((gs[-1:] * g0, hs[-1:]), yk)
            init = (jnp.ones((1, B, D, N), x.dtype), jnp.zeros((1, B, D, N), x.dtype))
            _, yc = jax.lax.scan(scan_chunk, init, (xc, bc, cc, dtc))
            return yc.transpose(2, 0, 1, 3).reshape(B, L, D)
        key = jax.random.key(seed)
        ks = jax.random.split(key, 6)
        x = jax.random.normal(ks[0], (B_SZ, L_SEQ, D_MODEL), dtype=jnp.float32)
        conv_w = jax.random.normal(ks[1], (CONV_K, D_MODEL), dtype=jnp.float32) / jnp.sqrt(3.0)
        W_bc = jax.random.normal(ks[2], (D_MODEL, 2 * N_STATE), dtype=jnp.float32) / jnp.sqrt(float(D_MODEL))
        b_bc = jnp.zeros((2 * N_STATE,), dtype=jnp.float32)
        W_dt = jax.random.normal(ks[3], (D_MODEL, DT_RANK), dtype=jnp.float32) / jnp.sqrt(float(D_MODEL))
        b_dt = jnp.zeros((DT_RANK,), dtype=jnp.float32)
        W_dtp = jax.random.normal(ks[4], (DT_RANK, D_MODEL), dtype=jnp.float32) / jnp.sqrt(float(DT_RANK))
        u0 = jax.random.uniform(ks[5], (D_MODEL,), dtype=jnp.float32, minval=DT_MIN, maxval=DT_MAX)
        b_dtp = _inverse_softplus(u0)
        A_log = jnp.log(jnp.tile(jnp.arange(1, N_STATE + 1, dtype=jnp.float32)[None, :], (D_MODEL, 1)))
        Dcoeff = jnp.ones((D_MODEL,), dtype=jnp.float32)
        return dict(x=x, conv_w=conv_w, W_bc=W_bc, b_bc=b_bc, W_dt=W_dt, b_dt=b_dt, W_dtp=W_dtp, b_dtp=b_dtp, A_log=A_log, Dcoeff=Dcoeff)
    _L0_attn_in = _L0_attn_setup()

    def _L0_ffn_setup():
        import jax, jax.numpy as jnp
        import numpy as np
        LN_EPS = 1e-05

        def layer_norm(x, g, b):
            mu = jnp.mean(x, axis=-1, keepdims=True)
            var = jnp.mean(jnp.square(x - mu), axis=-1, keepdims=True)
            return (x - mu) * jax.lax.rsqrt(var + LN_EPS) * g + b

        def ternary_quant(w):
            scale = 1.0 / jnp.clip(jnp.mean(jnp.abs(w)), 1e-05)
            wq = jnp.clip(jnp.round(w * scale), -1.0, 1.0) / scale
            return w + jax.lax.stop_gradient(wq - w)
        key = jax.random.key(seed)
        ks = jax.random.split(key, 3)
        dim, hidden = (128, 512)
        B, S = (8, 128)
        x = jax.random.normal(ks[0], (B, S, dim), dtype=jnp.float32)
        w1 = jax.random.normal(ks[1], (hidden, dim), dtype=jnp.float32) * 0.02
        w2 = jax.random.normal(ks[2], (dim, hidden), dtype=jnp.float32) * 0.02
        return {'x': x, 'ln1_g': jnp.ones((dim,), jnp.float32), 'ln1_b': jnp.zeros((dim,), jnp.float32), 'w1': w1, 'b1': jnp.zeros((hidden,), jnp.float32), 'ln2_g': jnp.ones((hidden,), jnp.float32), 'ln2_b': jnp.zeros((hidden,), jnp.float32), 'w2': w2, 'b2': jnp.zeros((dim,), jnp.float32)}
    _L0_ffn_in = _L0_ffn_setup()
    _d = {'L0_attn_x': _L0_attn_in['x'], 'L0_attn_conv_w': _L0_attn_in['conv_w'], 'L0_attn_W_bc': _L0_attn_in['W_bc'], 'L0_attn_b_bc': _L0_attn_in['b_bc'], 'L0_attn_W_dt': _L0_attn_in['W_dt'], 'L0_attn_b_dt': _L0_attn_in['b_dt'], 'L0_attn_W_dtp': _L0_attn_in['W_dtp'], 'L0_attn_b_dtp': _L0_attn_in['b_dtp'], 'L0_attn_A_log': _L0_attn_in['A_log'], 'L0_attn_Dcoeff': _L0_attn_in['Dcoeff'], 'L0_ffn_ln1_g': _L0_ffn_in['ln1_g'], 'L0_ffn_ln1_b': _L0_ffn_in['ln1_b'], 'L0_ffn_w1': _L0_ffn_in['w1'], 'L0_ffn_b1': _L0_ffn_in['b1'], 'L0_ffn_ln2_g': _L0_ffn_in['ln2_g'], 'L0_ffn_ln2_b': _L0_ffn_in['ln2_b'], 'L0_ffn_w2': _L0_ffn_in['w2'], 'L0_ffn_b2': _L0_ffn_in['b2']}
    _x0 = _d['L0_attn_x']
    _d['L0_attn_x'] = jax.random.normal(jax.random.fold_in(jax.random.key(seed), 1), (32, 256, 128), dtype=_x0.dtype)
    del _x0
    return _d

def reference(L0_attn_x, L0_attn_conv_w, L0_attn_W_bc, L0_attn_b_bc, L0_attn_W_dt, L0_attn_b_dt, L0_attn_W_dtp, L0_attn_b_dtp, L0_attn_A_log, L0_attn_Dcoeff, L0_ffn_ln1_g, L0_ffn_ln1_b, L0_ffn_w1, L0_ffn_b1, L0_ffn_ln2_g, L0_ffn_ln2_b, L0_ffn_w2, L0_ffn_b2):

    def _L0_attn_ref(x, conv_w, W_bc, b_bc, W_dt, b_dt, W_dtp, b_dtp, A_log, Dcoeff):
        import math
        import jax, jax.numpy as jnp
        import numpy as np
        B_SZ, L_SEQ, D_MODEL, N_STATE = (4, 512, 128, 16)
        DT_RANK = math.ceil(D_MODEL / 16)
        CONV_K = 3
        DT_MIN, DT_MAX = (0.001, 0.1)

        def _inverse_softplus(x):
            return x + jnp.log(1.0 - jnp.exp(-x))

        def _largest_factor_up_to(b, n):
            if n < 2:
                return n
            k = b
            while n % k != 0:
                k -= 1
            return k

        def _ssm_chunked_scan(x, A, Bc, Cc, dt):
            B, L, D = x.shape
            N = A.shape[-1]
            chunk = _largest_factor_up_to(int(math.sqrt(L)), L)
            nc = L // chunk
            r3 = lambda t, F: t.reshape(B, nc, chunk, F).transpose(1, 2, 0, 3)
            xc, dtc = (r3(x, D), r3(dt, D))
            bc, cc = (r3(Bc, N), r3(Cc, N))

            def assoc(lft, rgt):
                g_l, h_l = lft
                g_r, h_r = rgt
                return (g_l * g_r, g_r * h_l + h_r)

            def scan_chunk(carry, ch):
                g0, h0 = carry
                xk, bk, ck, dk = ch
                dA = jnp.exp(jnp.einsum('dn,lbd->lbdn', A, dk))
                dB = jnp.einsum('lbn,lbd,lbd->lbdn', bk, xk, dk)
                gs, hs = jax.lax.associative_scan(assoc, (dA, dB))
                hs = gs * h0 + hs
                yk = jnp.einsum('lbn,lbdn->lbd', ck, hs)
                return ((gs[-1:] * g0, hs[-1:]), yk)
            init = (jnp.ones((1, B, D, N), x.dtype), jnp.zeros((1, B, D, N), x.dtype))
            _, yc = jax.lax.scan(scan_chunk, init, (xc, bc, cc, dtc))
            return yc.transpose(2, 0, 1, 3).reshape(B, L, D)
        xp = jnp.pad(x, ((0, 0), (1, 1), (0, 0)))
        u = xp[:, :-2] * conv_w[0] + xp[:, 1:-1] * conv_w[1] + xp[:, 2:] * conv_w[2]
        u = jax.nn.silu(u)
        BC = u @ W_bc + b_bc
        Bcoeff, Ccoeff = jnp.split(BC, 2, axis=-1)
        A = -jnp.exp(A_log)
        dt = jax.nn.softplus((u @ W_dt + b_dt) @ W_dtp + b_dtp)
        y = _ssm_chunked_scan(x, A, Bcoeff, Ccoeff, dt)
        return y + x * Dcoeff

    def _L0_ffn_ref(x, ln1_g, ln1_b, w1, b1, ln2_g, ln2_b, w2, b2):
        import jax, jax.numpy as jnp
        import numpy as np
        LN_EPS = 1e-05

        def layer_norm(x, g, b):
            mu = jnp.mean(x, axis=-1, keepdims=True)
            var = jnp.mean(jnp.square(x - mu), axis=-1, keepdims=True)
            return (x - mu) * jax.lax.rsqrt(var + LN_EPS) * g + b

        def ternary_quant(w):
            scale = 1.0 / jnp.clip(jnp.mean(jnp.abs(w)), 1e-05)
            wq = jnp.clip(jnp.round(w * scale), -1.0, 1.0) / scale
            return w + jax.lax.stop_gradient(wq - w)
        h = layer_norm(x, ln1_g, ln1_b)
        h = jnp.einsum('bsd,hd->bsh', h, ternary_quant(w1)) + b1
        h = jax.nn.gelu(h, approximate=False)
        h = layer_norm(h, ln2_g, ln2_b)
        out = jnp.einsum('bsh,dh->bsd', h, ternary_quant(w2)) + b2
        return out
    x = L0_attn_x
    x = x + _L0_attn_ref(_layernorm(x, axis=-1), L0_attn_conv_w, L0_attn_W_bc, L0_attn_b_bc, L0_attn_W_dt, L0_attn_b_dt, L0_attn_W_dtp, L0_attn_b_dtp, L0_attn_A_log, L0_attn_Dcoeff)
    x = x + _L0_ffn_ref(_layernorm(x, axis=-1), L0_ffn_ln1_g, L0_ffn_ln1_b, L0_ffn_w1, L0_ffn_b1, L0_ffn_ln2_g, L0_ffn_ln2_b, L0_ffn_w2, L0_ffn_b2)
    return x

_drawn_inputs = setup_inputs


def setup_inputs(seed=0):
    import zlib

    import numpy as np

    out = dict(_drawn_inputs(seed))
    spreads = {'L0_attn_b_bc': (0.0, 0.426),
     'L0_attn_b_dt': (0.0, 0.8),
     'L0_attn_Dcoeff': (1.0, 0.2),
     'L0_ffn_ln1_g': (1.0, 0.6),
     'L0_ffn_ln1_b': (0.0, 0.604),
     'L0_ffn_b1': (0.0, 0.1),
     'L0_ffn_ln2_g': (1.0, 0.563),
     'L0_ffn_ln2_b': (0.0, 0.567),
     'L0_ffn_b2': (0.0, 0.1)}
    factors = {}
    for name, (base, spread) in spreads.items():
        noise = np.random.default_rng([zlib.crc32(name.encode()), seed]).standard_normal(out[name].shape)
        drawn = base * np.exp(spread * noise) if base else spread * noise
        out[name] = jnp.asarray(drawn.astype(out[name].dtype))
    for name, factor in factors.items():
        out[name] = (out[name] * factor).astype(out[name].dtype)
    return out
```

```python
from contextlib import ExitStack

import concourse.bass as bass
import concourse.mybir as mybir

F32 = mybir.dt.float32
BF16 = mybir.dt.bfloat16
ALU = mybir.AluOpType
ACT = mybir.ActivationFunctionType
AX = mybir.AxisListType

P = 128
SEQ = 256
NSTATE = 16
DSUB = P // NSTATE
CHUNK = 512
NB = CHUNK // SEQ
TT = CHUNK // P
QUAD = 4
BLOCKS = P // DSUB
PAIRS = BLOCKS // 2
ROUNDS_I = BLOCKS // QUAD
HID = 512
HC = HID // P
PARTS = 3
DECAY_BANKS = 3
EPS = 1e-5
SETUP_FIRST, SETUP_DVE = 8, 23
RINT = 1.5 * 2.0 ** 23

COLS = {}
_at = 0
for _name, _n in (("conv", 3), ("bB", 1), ("bC", 1), ("bdtp", 1), ("D", 1), ("g1", 1), ("lb1", 1),
                  ("b1", HC), ("g2", HC), ("lb2", HC), ("Alog", BLOCKS),
                  ("wB", P), ("wC", P), ("w1T", HID), ("w2T", HID)):
    COLS[_name] = (_at, _n)
    _at += _n
NCOLS = _at


def decay_bank(k):
    return k % DECAY_BANKS if k < BLOCKS - 1 else 1


def decay_before(k):
    for back in range(1, BLOCKS + 1):
        if decay_bank((k - back) % BLOCKS) == decay_bank(k):
            return back


class Item:

    def __init__(self, base, i=None):
        self.base, self.i = base, i

    def __add__(self, n):
        return Item(self.base + n, self.i)

    def times(self, per, plus):
        v = per * self.base + plus
        return v if self.i is None else self.i * (2 * per) + v

    def halves(self, per, plus):
        v = per * (self.base // 2) + plus
        return v if self.i is None else self.i * per + v


def wait(eng, sem, value):
    if isinstance(value, int) and value <= 0:
        return
    eng.wait_ge(sem, value)


def preln_ssm_ffn(nc, x, cols, dt_rows, b2_row, out, n_chunks):
    ctx = ExitStack()

    def sb(name, shape, dt=F32):
        return ctx.enter_context(nc.sbuf_tensor(name, shape, dt))

    def pb(name):
        return ctx.enter_context(nc.psum_tensor(name, [P, CHUNK], F32))

    def sem(name):
        return ctx.enter_context(nc.semaphore(name))

    with ctx:
        consts = sb("consts", [P, NCOLS])
        dtw = sb("dtw", [8, 2 * P + 1])
        b2r = sb("b2r", [1, P])
        ident = sb("ident", [P, P])
        ones = sb("ones", [P, P])
        avg = sb("avg", [P, P])
        minus_half = sb("minus_half", [P, TT])
        spread = sb("spread", [P, ROUNDS_I, P], BF16)
        gather = sb("gather", [P, ROUNDS_I, 32])
        diag_conv = sb("diag_conv", [P, 3, P])
        diag_D = sb("diag_D", [P, P])
        neg_a = sb("neg_a", [P, BLOCKS])
        w_pre = sb("w_pre", [P, P])
        b_pre = sb("b_pre", [P, 1])
        wtmp = sb("wtmp", [P, 2, HID])
        wq = sb("wq", [P, 2, HID])
        wsum = sb("wsum", [P, 2])
        wscale = sb("wscale", [P, 4])
        w1g = sb("w1g", [P, HID])
        bias1 = sb("bias1", [P, HC])
        w2g = sb("w2g", [P, HC, P])
        w2c = sb("w2c", [P, HC, P + 1])
        lb2m = sb("lb2m", [P, HC, P])
        const_row = sb("const_row", [P, P])

        def col(name):
            a, n = COLS[name]
            return consts[:, a:a + n]

        xf = sb("xf", [P, 2, TT, P])
        xb = sb("xb", [P, 2, TT, P])
        stats_f = sb("stats_f", [P, TT, 6])
        mom_f = sb("mom_f", [P, 7, TT])
        rstd_f = sb("rstd_f", [P, TT])
        z = sb("z", [P, TT, P])
        zT = sb("zT", [P, 2, NB, SEQ + 2])
        u = sb("u", [P, CHUNK])
        B_rep = sb("B_rep", [P, 2, CHUNK])
        C_rep = sb("C_rep", [P, 2, CHUNK])
        relu_pre = sb("relu_pre", [P, CHUNK])
        abs_pre = sb("abs_pre", [P, CHUNK])
        exp_pre = sb("exp_pre", [P, CHUNK])
        ln_pre = sb("ln_pre", [P, CHUNK])
        drive_in = sb("drive_in", [P, 2, CHUNK])
        rest = sb("rest", [P, 2, CHUNK])
        parts = sb("parts", [P, PARTS, 2, CHUNK], BF16)
        stacked = sb("stacked", [P, 2, QUAD, 2, CHUNK], BF16)
        driven = sb("driven", [P, 4, CHUNK])
        state = sb("state", [P, 4, 2, CHUNK])
        gated = sb("gated", [P, 4, QUAD, CHUNK])
        y_sb = sb("y_sb", [P, CHUNK])
        stats_b = sb("stats_b", [P, TT, 6])
        mom_b = sb("mom_b", [P, 7, TT])
        small_b = sb("small_b", [P, 7, TT])
        zz = sb("zz", [P, TT, P])
        zzT = sb("zzT", [P, CHUNK])
        x2c = sb("x2c", [P, TT, P])
        hid = sb("hid", [P, HC, CHUNK])
        hid_sq = sb("hid_sq", [P, HC, CHUNK])
        small_t = sb("small_t", [P, 2, 6, 2])
        ob = sb("ob", [P, 2, TT, P])

        decay = [pb(f"decay{n}") for n in range(DECAY_BANKS)]
        inflow = [pb(f"inflow{n}") for n in range(2)]
        y_ps = pb("y_ps")
        side = [pb("side0"), pb("side1")]

        s_consts = sem("consts_loaded")
        s_pool = sem("pool_setup")
        s_dve = sem("dve_setup")
        s_pe = sem("pe_setup")
        s_act = sem("act_setup")
        s_xf = [sem("xf_loaded0"), sem("xf_loaded1")]
        s_xb = [sem("xb_loaded0"), sem("xb_loaded1")]
        s_out = [sem("out_stored0"), sem("out_stored1")]
        s_stack = [sem("stacked0"), sem("stacked1")]
        s_fstat, s_frstd, s_z = sem("front_stats"), sem("front_rstd"), sem("z_ready")
        s_ztps, s_zt, s_conv, s_u = sem("zT_psum"), sem("zT_ready"), sem("conv_psum"), sem("u_ready")
        s_preps, s_bps, s_cps = sem("pre_psum"), sem("B_psum"), sem("C_psum")
        s_abs, s_exp, s_ln = sem("abs_ready"), sem("exp_ready"), sem("ln_ready")
        s_b, s_c = sem("B_ready"), sem("C_ready")
        s_dt, s_dtx = sem("dt_ready"), sem("dtx_ready")
        s_hi, s_mid, s_rest, s_lo = sem("hi_ready"), sem("mid_ready"), sem("rest_ready"), sem("lo_ready")
        s_dps, s_ips = sem("dt_spread"), sem("dtx_spread")
        s_decay, s_driven, s_state = sem("decay_ready"), sem("driven_ready"), sem("state_ready")
        s_gated, s_sum, s_skip = sem("gated_ready"), sem("quad_summed"), sem("skip_term")
        s_y, s_ytps, s_x2 = sem("y_ready"), sem("yT_psum"), sem("x2_ready")
        s_bstat, s_brstd, s_zz = sem("back_stats"), sem("back_rstd"), sem("zz_ready")
        s_zztps, s_zzt = sem("zzT_psum"), sem("zzT_ready")
        s_h1, s_gelu, s_sq = sem("hidden_psum"), sem("gelu_ready"), sem("square_ready")
        s_rr = sem("back_r_ready")
        s_x2c, s_h2 = sem("x2_const_ready"), sem("ffn_psum")
        s_tstat, s_trstd, s_res = sem("tail_stats"), sem("tail_rstd"), sem("result_ready")

        x_v = x.rearrange("(c n p) d -> c p n d", n=TT, p=P)
        out_v = out.rearrange("(c n p) d -> c p n d", n=TT, p=P)
        LAST = n_chunks - 1

        def chunk(view, item):
            if item.i is None:
                return view[item.base]
            return view[bass.ds(item.times(1, 0), 1)].rearrange("c p n d -> p (c n) d")

        def live(s, stage):
            return s.i is not None or 0 <= s.base + stage <= LAST

        FRONT, COEF, SCAN, BACK, TAIL = 2, 1, 0, -1, -2

        def steps(eng, setup_rest, step):
            for s in (-2, -1):
                step(Item(s))
            setup_rest()
            for s in (0, 1):
                step(Item(s))
            with eng.Fori(0, (n_chunks - 4) // 2) as i:
                for par in (0, 1):
                    step(Item(2 + par, i))
            for s in range(n_chunks - 2, n_chunks + 2):
                step(Item(s))

        block = ctx.enter_context(nc.Block())

        @block.sync
        def _(sp):
            for q in (0, 1):
                sp.sem_inc(s_out[q], 16)

            def load_front(h):
                q = h.base % 2
                wait(sp, s_z, h.times(1, -1))
                sp.dma_start(xf[:, q], chunk(x_v, h)).then_inc(s_xf[q], 16)

            sp.dma_start(consts[:, :], cols).then_inc(s_consts, 16)
            sp.dma_start(dtw[:, :], dt_rows).then_inc(s_consts, 16)
            sp.dma_start(b2r[:, :], b2_row).then_inc(s_consts, 16)

            def step(s):
                q = s.base % 2
                if live(s, SCAN):
                    h = s
                    wait(sp, s_x2c, h.times(1, -1))
                    wait(sp, s_zz, h.times(1, -1))
                    sp.dma_start(xb[:, q], chunk(x_v, h)).then_inc(s_xb[q], 16)
                if live(s, FRONT):
                    load_front(s + FRONT)
                if live(s, COEF):
                    h = s + 1
                    qh = h.base % 2
                    wait(sp, s_ips, h.times(BLOCKS, -BLOCKS))
                    wait(sp, s_mid, h.times(1, 1))
                    wait(sp, s_lo, h.times(1, 1))
                    for part in range(PARTS):
                        for j in range(QUAD):
                            sp.dma_start(stacked[32 * part:32 * part + 32, qh, j],
                                         parts[32 * j:32 * j + 32, part]).then_inc(s_stack[qh], 16)
                if live(s, TAIL):
                    h = s + TAIL
                    wait(sp, s_res, h.times(2, 2))
                    sp.dma_start(chunk(out_v, h), ob[:, h.base % 2]).then_inc(s_out[h.base % 2], 16)

            steps(sp, lambda: None, step)
            for q in (0, 1):
                sp.wait_ge(s_out[q], 16 + 16 * (n_chunks // 2))

        @block.gpsimd
        def _(pool):
            g = nc.gpsimd
            g.memset(ident[:, :], 0.0)
            g.memset(spread[:, :, :], 0.0)
            g.memset(gather[:, :, :], 0.0)
            g.memset(ones[:, :], 1.0)
            g.memset(minus_half[:, :], -0.5)
            g.memset(w2c[:, :, P:P + 1], 1.0)
            g.memset(avg[:, :], 1.0 / HID).then_inc(s_pool, 1)
            pool.wait_ge(s_pool, 1)
            g.affine_select(out=ident[:, :], in_=ident[:, :], compare_op=ALU.not_equal, fill=1.0,
                            base=0, pattern=[[-1, P]], channel_multiplier=1).then_inc(s_pool, 1)
            v = spread[0:96, :, :].rearrange("p i (n c) -> p i n c", c=DSUB)
            for part in range(PARTS):
                g.affine_select(out=v, in_=v, compare_op=ALU.not_equal, fill=1.0, base=-32 * part,
                                pattern=[[-DSUB, ROUNDS_I], [0, NSTATE], [-1, DSUB]],
                                channel_multiplier=1).then_inc(s_pool, 1)
                pool.wait_ge(s_pool, 3 + part)
            flat = gather[:, :, :].rearrange("p i d -> p (i d)")
            for n in range(NSTATE):
                for i in range(ROUNDS_I):
                    a = 32 * i + DSUB * i
                    w = flat[:, a:a + DSUB]
                    last = g.affine_select(out=w, in_=w, compare_op=ALU.not_equal, fill=1.0,
                                           base=-DSUB * n, pattern=[[-1, DSUB]], channel_multiplier=1)
                last.then_inc(s_pool, 1)
                pool.wait_ge(s_pool, 3 + PARTS + n)

            def step(s):
                q = s.base % 2
                h_f, h_c, h_b = s + FRONT, s + COEF, s + BACK

                def rstd_front():
                    wait(pool, s_fstat, h_f.times(5, 5))
                    g.tensor_tensor(rstd_f[:, :], mom_f[:, 6], minus_half[:, :], ALU.pow).then_inc(s_frstd, 1)

                def rstd_back(n):
                    wait(pool, s_bstat, h_b.times(8, 5 if n == 0 else 8))
                    g.tensor_tensor(small_b[:, 1 if n == 0 else 5], mom_b[:, 6] if n == 0 else small_b[:, 4],
                                    minus_half[:, :], ALU.pow).then_inc(s_brstd, 1)

                def rstd_tail(a):
                    wait(pool, s_tstat, (s + TAIL).times(8, 4 * a + 4))
                    g.tensor_tensor(small_t[:, a, 5], small_t[:, a, 4], minus_half[:, 0:2],
                                    ALU.pow).then_inc(s_trstd, 1)

                def residue():
                    wait(pool, s_hi, h_c.times(1, 1))
                    g.tensor_tensor(rest[:, :, :], drive_in[:, :, :], parts[:, 0], ALU.subtract).then_inc(s_rest, 1)

                def low_part():
                    wait(pool, s_mid, h_c.times(1, 1))
                    g.tensor_tensor(parts[:, 2], rest[:, :, :], parts[:, 1], ALU.subtract).then_inc(s_lo, 1)

                for pair in range(PAIRS):
                    if live(s, SCAN):
                        wait(pool, s_state, s.times(BLOCKS, 2 * pair + 2))
                        if pair % 2 == 0:
                            wait(pool, s_sum, s.times(ROUNDS_I, pair // 2 + 1 - 4))
                        if pair == 0:
                            wait(pool, s_c, s.times(1, 1))
                        g.tensor_tensor(
                            gated[:, pair // 2, 2 * (pair % 2):2 * (pair % 2) + 2, :],
                            state[:, pair % 4, :, :],
                            C_rep[:, q, :].unsqueeze(1).broadcast_to([P, 2, CHUNK]),
                            ALU.mult).then_inc(s_gated, 1)
                    if pair == 0 and live(s, FRONT):
                        rstd_front()
                    if pair == 1 and live(s, TAIL):
                        rstd_tail(0)
                    if pair == 2 and live(s, COEF):
                        residue()
                    if pair == 3 and live(s, TAIL):
                        rstd_tail(1)
                    if pair == 3 and live(s, COEF):
                        low_part()
                    if pair == 4 and live(s, BACK):
                        rstd_back(0)
                    if pair == 5 and live(s, BACK):
                        rstd_back(1)
                        wait(pool, s_res, h_b.times(2, 0))
                        wait(pool, s_x2, h_b.times(1, 1))
                        g.tensor_tensor(x2c[:, :, :], xb[:, h_b.base % 2],
                                        const_row[:, :].unsqueeze(1).broadcast_to([P, TT, P]),
                                        ALU.add).then_inc(s_x2c, 1)

            steps(pool, lambda: pool.wait_ge(s_dve, SETUP_DVE), step)

        @block.scalar
        def _(act):
            a = nc.scalar
            act.wait_ge(s_consts, 48)
            a.activation(neg_a[:, :], col("Alog"), ACT.Exp).then_inc(s_act, 1)
            act.wait_ge(s_act, 1)
            a.activation(neg_a[:, :], neg_a[:, :], ACT.Copy, scale=-1.0).then_inc(s_act, 1)
            act.wait_ge(s_act, 2)

            def step(s):
                q = s.base % 2
                h_f, h_c, h_b = s + FRONT, s + COEF, s + BACK
                qf, qc = h_f.base % 2, h_c.base % 2

                def exp_block(k):
                    wait(act, s_dps, s.times(BLOCKS, k + 1))
                    v = decay[decay_bank(k)][:, :].rearrange("p (b t) -> p b t", b=NB)[:, :, 1:]
                    a.activation(v, v, ACT.Exp, scale=neg_a[:, k:k + 1]).then_inc(s_decay, 1)

                def pre_parts():
                    wait(act, s_preps, h_c.times(1, 1))
                    wait(act, s_dt, h_c.times(1, 0))
                    a.activation(relu_pre[:, :], side[0][:, :], ACT.Relu, bias=b_pre[:, 0:1])
                    a.activation(abs_pre[:, :], side[0][:, :], ACT.Abs, bias=b_pre[:, 0:1]).then_inc(s_abs, 1)

                def pre_exp():
                    wait(act, s_abs, h_c.times(1, 1))
                    a.activation(exp_pre[:, :], abs_pre[:, :], ACT.Exp, scale=-1.0).then_inc(s_exp, 1)

                def pre_ln():
                    wait(act, s_exp, h_c.times(1, 1))
                    a.activation(ln_pre[:, :], exp_pre[:, :], ACT.Ln, bias=1.0).then_inc(s_ln, 1)

                def copy_B():
                    wait(act, s_bps, h_c.times(1, 1))
                    wait(act, s_driven, h_c.times(BLOCKS, -BLOCKS))
                    a.activation(B_rep[:, qc], side[1][:, :], ACT.Identity, bias=col("bB")).then_inc(s_b, 1)

                def copy_C():
                    wait(act, s_cps, h_c.times(1, 1))
                    wait(act, s_gated, h_c.times(PAIRS, -PAIRS))
                    a.activation(C_rep[:, qc], side[0][:, :], ACT.Identity, bias=col("bC")).then_inc(s_c, 1)

                def hi_part():
                    wait(act, s_dtx, h_c.times(1, 1))
                    if h_c.i is not None or h_c.base > 0:
                        wait(act, s_stack[1 - qc], (h_c + -1).halves(16 * 12, 16 * 12))
                    a.copy(parts[:, 0], drive_in[:, :, :]).then_inc(s_hi, 1)

                def mid_part():
                    wait(act, s_rest, h_c.times(1, 1))
                    a.copy(parts[:, 1], rest[:, :, :]).then_inc(s_mid, 1)

                def copy_y():
                    wait(act, s_sum, h_b.times(ROUNDS_I, ROUNDS_I))
                    wait(act, s_ytps, h_b.times(1, 0))
                    a.copy(y_sb[:, :], y_ps[:, :]).then_inc(s_y, 1)

                def copy_zT():
                    wait(act, s_ztps, h_f.times(1, 1))
                    wait(act, s_skip, h_f.times(1, -1))
                    wait(act, s_dtx, h_f.times(1, -1))
                    a.copy(zT[:, qf, :, 1:SEQ + 1],
                           side[0][:, :].rearrange("p (b t) -> p b t", b=NB)).then_inc(s_zt, 1)

                def copy_zzT():
                    wait(act, s_zztps, h_b.times(1, 1))
                    wait(act, s_h1, h_b.times(HC, 0))
                    a.copy(zzT[:, :], side[1][:, :]).then_inc(s_zzt, 1)

                def silu():
                    wait(act, s_conv, h_f.times(1, 1))
                    wait(act, s_cps, h_f.times(1, 0))
                    a.activation(u[:, :], side[0][:, :], ACT.Silu).then_inc(s_u, 1)

                def gelu(c):
                    wait(act, s_h1, h_b.times(HC, c + 1))
                    if c == 0:
                        wait(act, s_h2, h_b.times(2, 0))
                    a.activation(hid[:, c], side[(c + 1) % 2][:, :], ACT.Gelu,
                                 bias=bias1[:, c:c + 1]).then_inc(s_gelu, 1)

                def square(n):
                    wait(act, s_gelu, h_b.times(HC, 2 * n + 2))
                    a.activation(hid_sq[:, 2 * n:2 * n + 2], hid[:, 2 * n:2 * n + 2],
                                 ACT.Square).then_inc(s_sq, 1)

                for k in range(BLOCKS):
                    if live(s, SCAN):
                        exp_block(k)
                    if live(s, COEF):
                        if k == 0:
                            pre_parts()
                        if k == 1:
                            pre_exp()
                            copy_B()
                        if k == 2:
                            pre_ln()
                        if k == 3:
                            copy_C()
                        if k == 6:
                            hi_part()
                        if k == 9:
                            mid_part()
                    if k == 8 and live(s, BACK):
                        copy_y()
                    if k == 11 and live(s, FRONT):
                        copy_zT()
                    if k == 14 and live(s, BACK):
                        copy_zzT()
                    if k == 15:
                        if live(s, FRONT):
                            silu()
                        if live(s, BACK):
                            for c in range(HC):
                                gelu(c)
                            square(0)
                            square(1)

            def rest_of_setup():
                act.wait_ge(s_dve, SETUP_DVE)

            act.wait_ge(s_dve, SETUP_FIRST)
            steps(act, rest_of_setup, step)

        @block.vector
        def _(dve):
            v = nc.vector
            done = [0]

            def link(ins):
                done[0] += 1
                ins.then_inc(s_dve, 1)
                dve.wait_ge(s_dve, done[0])

            for n in range(DECAY_BANKS):
                v.memset(decay[n][:, :], 0.0)
            link(v.memset(zT[:, :, :, :], 0.0))
            dve.wait_ge(s_consts, 48)
            dve.wait_ge(s_pool, 2)
            for n in range(3):
                link(v.tensor_scalar(diag_conv[:, n], ident[:, :], col("conv")[:, n:n + 1], None, ALU.mult))
            link(v.tensor_scalar(diag_D[:, :], ident[:, :], col("D"), None, ALU.mult))
            dve.wait_ge(s_pe, 1)
            link(v.tensor_copy(w_pre[:, :], y_ps[:, 0:P]))
            link(v.tensor_tensor(b_pre[:, :], y_ps[:, P:P + 1], col("bdtp"), ALU.add))
            link(v.memset(small_t[:, :, :, :], 0.0))
            assert done[0] == SETUP_FIRST

            def rest_of_setup():
                w_raw = consts[:, COLS["w1T"][0]:COLS["w1T"][0] + 2 * HID].rearrange("p (a n) -> p a n", a=2)
                link(v.scalar_tensor_tensor(wtmp[:, :, :], w_raw, -1.0, w_raw, ALU.mult, ALU.max))
                link(v.reduce_sum(wsum[:, :], wtmp[:, :, :], AX.X))
                dve.wait_ge(s_pe, 2)
                link(v.tensor_scalar(wscale[:, 0:2], y_ps[:, 0:2], 1.0 / (HID * P), 1e-5, ALU.mult, ALU.max))
                link(v.reciprocal(wscale[:, 2:4], wscale[:, 0:2]))
                link(v.reciprocal(wscale[:, 0:2], wscale[:, 2:4]))
                for m in range(2):
                    v.tensor_scalar(wtmp[:, m], w_raw[:, m], wscale[:, 2 + m:3 + m], 1.0, ALU.mult, ALU.min)
                link(v.memset(small_t[:, :, :, :], 0.0))
                link(v.tensor_scalar(wq[:, :, :], wtmp[:, :, :], -1.0, RINT, ALU.max, ALU.add))
                link(v.tensor_scalar(wtmp[:, :, :], wq[:, :, :], RINT, None, ALU.subtract))
                for m in range(2):
                    last = v.scalar_tensor_tensor(wq[:, m], wtmp[:, m], wscale[:, m:m + 1], w_raw[:, m],
                                                  ALU.mult, ALU.subtract)
                link(last)
                link(v.tensor_tensor(wq[:, :, :], wq[:, :, :], w_raw, ALU.add))
                link(v.tensor_scalar(w1g[:, :], wq[:, 0], col("g1"), None, ALU.mult))
                for c in range(HC):
                    v.tensor_scalar(w2g[:, c], wq[:, 1, c * P:(c + 1) * P], col("g2")[:, c:c + 1], None, ALU.mult)
                    last = v.tensor_scalar(lb2m[:, c], ones[:, :], col("lb2")[:, c:c + 1], None, ALU.mult)
                link(last)
                dve.wait_ge(s_pe, 3)
                link(v.tensor_tensor(bias1[:, :], y_ps[:, 4:4 + HC], col("b1"), ALU.add))
                link(v.tensor_copy(const_row[:, :], y_ps[:, 2 * P:3 * P]))
                for c in range(HC):
                    last = v.tensor_tensor(w2c[:, c, 0:P], w2g[:, c], y_ps[:, P:2 * P], ALU.subtract)
                link(last)
                assert done[0] == SETUP_DVE, done

            def step(s):
                q = s.base % 2
                h_f, h_c, h_b, h_t = s + FRONT, s + COEF, s + BACK, s + TAIL
                qf, qc, qb, qt = (h.base % 2 for h in (h_f, h_c, h_b, h_t))

                def scan_block(k):
                    wait(dve, s_ips, s.times(BLOCKS, k + 1))
                    if k == 0:
                        wait(dve, s_b, s.times(1, 1))
                    v.tensor_tensor(driven[:, k % 4], inflow[k % 2][:, :], B_rep[:, q],
                                    ALU.mult).then_inc(s_driven, 1)
                    wait(dve, s_decay, s.times(BLOCKS, k + 1))
                    wait(dve, s_driven, s.times(BLOCKS, k + 1))
                    if k % 2 == 0:
                        wait(dve, s_gated, s.times(PAIRS, k // 2 + 1 - 4))
                    v.tensor_tensor_scan(state[:, (k // 2) % 4, k % 2], decay[decay_bank(k)][:, :],
                                         driven[:, k % 4], 0.0, ALU.mult, ALU.add).then_inc(s_state, 1)

                def moments(stats, m, done, h, per):
                    wait(dve, done, h.times(per, 1))
                    v.tensor_tensor(m[:, 0], stats[:, :, 1], stats[:, :, 4], ALU.add)
                    v.tensor_tensor(m[:, 1], stats[:, :, 1], stats[:, :, 4], ALU.subtract)
                    v.tensor_tensor(m[:, 2], stats[:, :, 2], stats[:, :, 5], ALU.add).then_inc(done, 1)
                    wait(dve, done, h.times(per, 2))
                    v.tensor_scalar(m[:, 4], m[:, 0], 0.5, None, ALU.mult)
                    v.scalar_tensor_tensor(m[:, 3], m[:, 1], 0.25, m[:, 1], ALU.mult, ALU.mult).then_inc(done, 1)
                    wait(dve, done, h.times(per, 3))
                    v.scalar_tensor_tensor(m[:, 5], m[:, 2], 1.0 / P, m[:, 3], ALU.mult, ALU.add).then_inc(done, 1)
                    wait(dve, done, h.times(per, 4))
                    v.tensor_scalar(m[:, 6], m[:, 5], EPS, None, ALU.add).then_inc(done, 1)

                def front_stats():
                    wait(dve, s_xf[qf], h_f.halves(16, 16))
                    for n in range(TT):
                        last = v.bn_stats(stats_f[:, n], xf[:, qf, n])
                    last.then_inc(s_fstat, 1)
                    moments(stats_f, mom_f, s_fstat, h_f, 5)

                def front_z():
                    wait(dve, s_frstd, h_f.times(1, 1))
                    wait(dve, s_ztps, h_f.times(1, 0))
                    for n in range(TT):
                        last = v.tensor_scalar(z[:, n], xf[:, qf, n], mom_f[:, 4, n:n + 1], rstd_f[:, n:n + 1],
                                               ALU.subtract, ALU.mult)
                    last.then_inc(s_z, 1)

                def dt_parts():
                    wait(dve, s_ln, h_c.times(1, 1))
                    wait(dve, s_rest, h_c.times(1, 0))
                    wait(dve, s_zt, h_c.times(1, 1))
                    v.tensor_tensor(drive_in[:, 0], relu_pre[:, :], ln_pre[:, :], ALU.add).then_inc(s_dt, 1)
                    wait(dve, s_dt, h_c.times(1, 1))
                    v.tensor_tensor(drive_in[:, 1].rearrange("p (b t) -> p b t", b=NB),
                                    drive_in[:, 0].rearrange("p (b t) -> p b t", b=NB),
                                    zT[:, qc, :, 1:SEQ + 1], ALU.mult).then_inc(s_dtx, 1)

                def back_residual():
                    wait(dve, s_ytps, h_b.times(1, 1))
                    wait(dve, s_xb[qb], h_b.halves(16, 16))
                    v.tensor_tensor(xb[:, qb], xb[:, qb],
                                    side[1][:, :].rearrange("p (n d) -> p n d", n=TT),
                                    ALU.add).then_inc(s_x2, 1)
                    wait(dve, s_x2, h_b.times(1, 1))
                    for n in range(TT):
                        last = v.bn_stats(stats_b[:, n], xb[:, qb, n])
                    last.then_inc(s_bstat, 1)
                    moments(stats_b, mom_b, s_bstat, h_b, 8)

                def back_second_norm():
                    wait(dve, s_brstd, h_b.times(2, 1))
                    v.tensor_tensor(small_b[:, 2], mom_b[:, 5], small_b[:, 1], ALU.mult).then_inc(s_bstat, 1)
                    wait(dve, s_bstat, h_b.times(8, 6))
                    v.tensor_tensor(small_b[:, 3], small_b[:, 2], small_b[:, 1], ALU.mult).then_inc(s_bstat, 1)
                    wait(dve, s_bstat, h_b.times(8, 7))
                    v.tensor_scalar(small_b[:, 4], small_b[:, 3], EPS, None, ALU.add).then_inc(s_bstat, 1)

                def back_zz():
                    wait(dve, s_brstd, h_b.times(2, 2))
                    v.tensor_tensor(small_b[:, 6], small_b[:, 1], small_b[:, 5], ALU.mult).then_inc(s_rr, 1)
                    wait(dve, s_rr, h_b.times(1, 1))
                    wait(dve, s_zztps, h_b.times(1, 0))
                    for n in range(TT):
                        last = v.tensor_scalar(zz[:, n], xb[:, qb, n], mom_b[:, 4, n:n + 1], small_b[:, 6, n:n + 1],
                                               ALU.subtract, ALU.mult)
                    last.then_inc(s_zz, 1)

                def bank_tail(a):
                    return side[1 - a][:, :].rearrange("p (t c) -> p t c", t=2)

                def tail_stats(a):
                    m = small_t[:, a]
                    wait(dve, s_h2, h_t.times(2, a + 1))
                    v.tensor_scalar(m[:, 0], bank_tail(a)[:, :, P], 1.0 / HID, None, ALU.mult).then_inc(s_tstat, 1)
                    wait(dve, s_tstat, h_t.times(8, 4 * a + 1))
                    v.tensor_tensor(m[:, 1], m[:, 0], m[:, 0], ALU.mult).then_inc(s_tstat, 1)
                    wait(dve, s_tstat, h_t.times(8, 4 * a + 2))
                    v.scalar_tensor_tensor(m[:, 2], bank_tail(a)[:, :, P + 1], 1.0 / HID, m[:, 1],
                                           ALU.mult, ALU.subtract).then_inc(s_tstat, 1)
                    wait(dve, s_tstat, h_t.times(8, 4 * a + 3))
                    v.tensor_scalar(m[:, 4], m[:, 2], 0.0, EPS, ALU.max, ALU.add).then_inc(s_tstat, 1)

                def tail_result(a):
                    if a == 0:
                        wait(dve, s_x2c, h_t.times(1, 1))
                        wait(dve, s_out[qt], h_t.halves(16, 16))
                    wait(dve, s_trstd, h_t.times(2, a + 1))
                    for t in range(2):
                        n = 2 * a + t
                        last = v.scalar_tensor_tensor(ob[:, qt, n], bank_tail(a)[:, t, 0:P],
                                                      small_t[:, a, 5, t:t + 1], x2c[:, n],
                                                      ALU.mult, ALU.add)
                    last.then_inc(s_res, 1)

                for k in range(BLOCKS):
                    if live(s, SCAN):
                        scan_block(k)
                    if k == 0 and live(s, FRONT):
                        front_stats()
                    if k == 2 and live(s, FRONT):
                        front_z()
                    if live(s, COEF) and k == 2:
                        dt_parts()
                    if live(s, TAIL):
                        if k == 4:
                            tail_stats(0)
                        if k == 6:
                            tail_result(0)
                            tail_stats(1)
                        if k == 8:
                            tail_result(1)
                    if live(s, BACK):
                        if k == 8:
                            back_residual()
                        if k == 10:
                            back_second_norm()
                        if k == 12:
                            back_zz()

            steps(dve, rest_of_setup, step)

        @block.tensor
        def _(pe):
            mm = nc.tensor.matmul
            pe.wait_ge(s_consts, 48)
            mm(y_ps[:, 0:P], dtw[:, 0:P], dtw[:, P:2 * P], start=True, stop=True)
            mm(y_ps[:, P:P + 1], dtw[:, P:2 * P], dtw[:, 2 * P:2 * P + 1], start=True, stop=True).then_inc(s_pe, 1)
            pe.wait_ge(s_pool, 2 + PARTS + NSTATE)
            pe.wait_ge(s_dve, SETUP_FIRST)

            def rest_of_setup():
                pe.wait_ge(s_dve, SETUP_FIRST + 2)
                mm(y_ps[:, 0:2], ones[:, :], wsum[:, :], start=True, stop=True).then_inc(s_pe, 1)
                pe.wait_ge(s_dve, SETUP_DVE - 3)
                for c in range(HC):
                    mm(y_ps[:, 4 + c:5 + c], wq[:, 0, c * P:(c + 1) * P], col("lb1"), start=True, stop=True)
                for c in range(HC):
                    mm(y_ps[:, P:2 * P], avg[:, :], w2g[:, c], start=(c == 0), stop=(c == HC - 1))
                for c in range(HC):
                    mm(y_ps[:, 2 * P:3 * P], lb2m[:, c], wq[:, 1, c * P:(c + 1) * P], start=(c == 0), stop=False)
                mm(y_ps[:, 2 * P:3 * P], ones[0:1, :], b2r[:, :], start=False, stop=True).then_inc(s_pe, 1)
                pe.wait_ge(s_dve, SETUP_DVE)

            def step(s):
                q = s.base % 2
                h_f, h_c, h_b, h_t = s + FRONT, s + COEF, s + BACK, s + TAIL
                qf = h_f.base % 2

                def spread_block(k):
                    i, j = k // QUAD, k % QUAD
                    if k == 0:
                        wait(pe, s_stack[q], s.halves(16 * 12, 16 * 12))
                    wait(pe, s_state, s.times(BLOCKS, k + 1 - decay_before(k)))
                    mm(decay[decay_bank(k)][:, :].rearrange("p (b t) -> p b t", b=NB)[:, :, 1:],
                       spread[0:96, i], stacked[0:96, q, j, 0].rearrange("p (b t) -> p b t", b=NB)[:, :, 1:],
                       start=True, stop=True).then_inc(s_dps, 1)
                    wait(pe, s_driven, s.times(BLOCKS, k + 1 - 2))
                    mm(inflow[k % 2][:, :], spread[0:96, i], stacked[0:96, q, j, 1],
                       start=True, stop=True).then_inc(s_ips, 1)

                def sum_quad(m, i):
                    wait(pe, s_gated, m.times(PAIRS, 2 * i + 2))
                    for j in range(QUAD):
                        last = mm(y_ps[32 * j:32 * j + 32, :], gather[:, i], gated[:, i, j],
                                  start=False, stop=(i == ROUNDS_I - 1), skip_group_check=True)
                    last.then_inc(s_sum, 1)

                def skip_term():
                    wait(pe, s_y, s.times(1, 0))
                    mm(y_ps[:, :].rearrange("p (b t) -> p b t", b=NB), diag_D[:, :], zT[:, q, :, 1:SEQ + 1],
                       start=True, stop=False, skip_group_check=True).then_inc(s_skip, 1)

                def pre():
                    wait(pe, s_u, h_c.times(1, 1))
                    wait(pe, s_gelu, h_c.times(HC, -3 * HC + 4))
                    mm(side[0][:, :], w_pre[:, :], u[:, :], start=True, stop=True).then_inc(s_preps, 1)

                def fill_B():
                    wait(pe, s_gelu, h_c.times(HC, -3 * HC + 3))
                    mm(side[1][:, :], col("wB"), u[:, :], start=True, stop=True).then_inc(s_bps, 1)

                def fill_C():
                    wait(pe, s_abs, h_c.times(1, 1))
                    mm(side[0][:, :], col("wC"), u[:, :], start=True, stop=True).then_inc(s_cps, 1)

                def second(a):
                    wait(pe, s_sq, h_t.times(2, 2))
                    if a == 0 and live(s, COEF):
                        wait(pe, s_b, h_c.times(1, 1))
                    if a == 1 and live(s, COEF):
                        wait(pe, s_c, h_c.times(1, 1))
                    bank = side[1 - a][:, :].rearrange("p (t c) -> p t c", t=2)
                    for t in range(2):
                        tok = slice(P * (2 * a + t), P * (2 * a + t) + P)
                        for c in range(HC):
                            mm(bank[:, t, 0:P + 1], hid[:, c, tok], w2c[:, c], start=(c == 0), stop=(c == HC - 1))
                        for c in range(HC):
                            last = mm(bank[:, t, P + 1:P + 2], hid_sq[:, c, tok], ones[:, 0:1],
                                      start=(c == 0), stop=(c == HC - 1))
                    last.then_inc(s_h2, 1)

                def transpose_y():
                    wait(pe, s_y, h_b.times(1, 1))
                    if live(s, TAIL):
                        wait(pe, s_res, h_t.times(2, 1))
                    elif live(s, COEF):
                        wait(pe, s_b, h_c.times(1, 1))
                    for n in range(TT):
                        last = nc.tensor.transpose(side[1][:, n * P:(n + 1) * P], y_sb[:, n * P:(n + 1) * P], ident[:, :])
                    last.then_inc(s_ytps, 1)

                def transpose_z():
                    wait(pe, s_z, h_f.times(1, 1))
                    if live(s, TAIL):
                        wait(pe, s_res, h_t.times(2, 2))
                    elif live(s, COEF):
                        wait(pe, s_c, h_c.times(1, 1))
                    for n in range(TT):
                        last = nc.tensor.transpose(side[0][:, n * P:(n + 1) * P], z[:, n], ident[:, :])
                    last.then_inc(s_ztps, 1)

                def convolve():
                    wait(pe, s_zt, h_f.times(1, 1))
                    for n in range(3):
                        last = mm(side[0][:, :].rearrange("p (b t) -> p b t", b=NB), diag_conv[:, n],
                                  zT[:, qf, :, n:n + SEQ], start=(n == 0), stop=(n == 2))
                    last.then_inc(s_conv, 1)

                def transpose_zz():
                    wait(pe, s_zz, h_b.times(1, 1))
                    for n in range(TT):
                        last = nc.tensor.transpose(side[1][:, n * P:(n + 1) * P], zz[:, n], ident[:, :])
                    last.then_inc(s_zztps, 1)

                def first(c):
                    if c == 0:
                        wait(pe, s_zzt, h_b.times(1, 1))
                    elif c == 1:
                        if live(s, FRONT):
                            wait(pe, s_u, h_f.times(1, 1))
                        elif live(s, TAIL):
                            wait(pe, s_res, h_t.times(2, 2))
                    else:
                        wait(pe, s_gelu, h_b.times(HC, c - 1))
                    mm(side[(c + 1) % 2][:, :], w1g[:, c * P:(c + 1) * P], zzT[:, :],
                       start=True, stop=True).then_inc(s_h1, 1)

                for k in range(BLOCKS):
                    if live(s, SCAN):
                        spread_block(k)
                    if live(s, COEF):
                        if k == 0:
                            pre()
                        if k == 2:
                            fill_B()
                        if k == 3:
                            fill_C()
                    if live(s, BACK):
                        if k == 1:
                            sum_quad(h_b, 2)
                        if k == 5:
                            sum_quad(h_b, 3)
                    if live(s, TAIL):
                        if k == 4:
                            second(0)
                        if k == 6:
                            second(1)
                    if k == 8 and live(s, BACK):
                        transpose_y()
                    if k == 8 and live(s, SCAN):
                        skip_term()
                    if k == 11 and live(s, FRONT):
                        transpose_z()
                    if k == 9 and live(s, SCAN):
                        sum_quad(s, 0)
                    if k == 12 and live(s, FRONT):
                        convolve()
                    if k == 13 and live(s, SCAN):
                        sum_quad(s, 1)
                    if k == 14 and live(s, BACK):
                        transpose_zz()
                    if k == 15 and live(s, BACK):
                        for c in range(HC):
                            first(c)

            steps(pe, rest_of_setup, step)


def kernel(**inputs):
    import numpy as np
    import concourse.bacc as bacc
    from concourse.bass_utils import run_bass_kernel_spmd

    a = {k: np.asarray(v) for k, v in inputs.items()}
    f = lambda name: a["L0_" + name]
    xs = f("attn_x")
    tokens = xs.shape[0] * xs.shape[1]
    a_log = f("attn_A_log").reshape(QUAD, ROUNDS_I, DSUB, NSTATE).transpose(3, 2, 1, 0).reshape(P, BLOCKS)
    w_bc, b_bc = f("attn_W_bc"), f("attn_b_bc")
    packed = {
        "conv": f("attn_conv_w").T,
        "bB": np.repeat(b_bc[:NSTATE], DSUB)[:, None], "bC": np.repeat(b_bc[NSTATE:], DSUB)[:, None],
        "bdtp": f("attn_b_dtp")[:, None], "D": f("attn_Dcoeff")[:, None],
        "g1": f("ffn_ln1_g")[:, None], "lb1": f("ffn_ln1_b")[:, None],
        "b1": f("ffn_b1").reshape(HC, P).T, "g2": f("ffn_ln2_g").reshape(HC, P).T,
        "lb2": f("ffn_ln2_b").reshape(HC, P).T, "Alog": a_log,
        "wB": np.repeat(w_bc[:, :NSTATE], DSUB, axis=1), "wC": np.repeat(w_bc[:, NSTATE:], DSUB, axis=1),
        "w1T": f("ffn_w1").T,
        "w2T": f("ffn_w2").T.reshape(HC, P, P).transpose(1, 0, 2).reshape(P, HID),
    }
    arrays = {
        "x": np.ascontiguousarray(xs.reshape(tokens, P)),
        "cols": np.ascontiguousarray(np.concatenate([packed[k] for k in COLS], axis=1)),
        "dt_rows": np.ascontiguousarray(np.concatenate(
            [f("attn_W_dt").T, f("attn_W_dtp"), f("attn_b_dt")[:, None]], axis=1)),
        "b2_row": np.ascontiguousarray(f("ffn_b2")[None, :]),
    }
    nc = bacc.Bacc("TRN2", target_bir_lowering=False, num_devices=1)
    aps = [nc.dram_tensor(k, v.shape, mybir.dt.from_np(v.dtype), kind="ExternalInput").ap()
           for k, v in arrays.items()]
    out = nc.dram_tensor("out", (tokens, P), F32, kind="ExternalOutput").ap()
    preln_ssm_ffn(nc, *aps, out, tokens // CHUNK)
    r = run_bass_kernel_spmd(nc, [arrays], core_ids=[0])
    return r.results[0]["out"].reshape(xs.shape)
```

```python
from contextlib import ExitStack

import concourse.bass as bass
import concourse.mybir as mybir

F32 = mybir.dt.float32
BF16 = mybir.dt.bfloat16
ALU = mybir.AluOpType
ACT = mybir.ActivationFunctionType
AX = mybir.AxisListType

P = 128
SEQ = 256
NSTATE = 16
DSUB = P // NSTATE
CHUNK = 512
NB = CHUNK // SEQ
TT = CHUNK // P
QUAD = 4
BLOCKS = P // DSUB
PAIRS = BLOCKS // 2
ROUNDS_I = BLOCKS // QUAD
HID = 512
HC = HID // P
PARTS = 3
DECAY_BANKS = 3
EPS = 1e-5
SETUP_FIRST, SETUP_DVE = 9, 24
RINT = 1.5 * 2.0 ** 23

COLS = {}
_at = 0
for _name, _n in (("conv", 3), ("bB", 1), ("bC", 1), ("bdtp", 1), ("D", 1), ("g1", 1), ("lb1", 1),
                  ("b1", HC), ("g2", HC), ("lb2", HC), ("Alog", BLOCKS),
                  ("wB", P), ("wC", P), ("w1T", HID), ("w2T", HID)):
    COLS[_name] = (_at, _n)
    _at += _n
NCOLS = _at


def decay_bank(k):
    return k % DECAY_BANKS if k < BLOCKS - 1 else 1


def decay_before(k):
    for back in range(1, BLOCKS + 1):
        if decay_bank((k - back) % BLOCKS) == decay_bank(k):
            return back


class Item:

    def __init__(self, base, i=None):
        self.base, self.i = base, i

    def __add__(self, n):
        return Item(self.base + n, self.i)

    def times(self, per, plus):
        v = per * self.base + plus
        return v if self.i is None else self.i * (2 * per) + v

    def halves(self, per, plus):
        v = per * (self.base // 2) + plus
        return v if self.i is None else self.i * per + v


def wait(eng, sem, value):
    if isinstance(value, int) and value <= 0:
        return
    eng.wait_ge(sem, value)


def preln_ssm_ffn(nc, x, cols, dt_rows, b2_row, out, n_chunks):
    ctx = ExitStack()

    def sb(name, shape, dt=F32):
        return ctx.enter_context(nc.sbuf_tensor(name, shape, dt))

    def pb(name):
        return ctx.enter_context(nc.psum_tensor(name, [P, CHUNK], F32))

    def sem(name):
        return ctx.enter_context(nc.semaphore(name))

    with ctx:
        consts = sb("consts", [P, NCOLS])
        dtw = sb("dtw", [8, 2 * P + 1])
        b2r = sb("b2r", [1, P])
        ident = sb("ident", [P, P])
        ones = sb("ones", [P, P])
        avg = sb("avg", [P, P])
        pick_sum = sb("pick_sum", [P, 2, 32])
        pick_row = sb("pick_row", [P, 2])
        minus_half = sb("minus_half", [P, TT])
        spread = sb("spread", [P, ROUNDS_I, P], BF16)
        gather = sb("gather", [P, ROUNDS_I, 32])
        diag_conv = sb("diag_conv", [P, 3, P])
        diag_D = sb("diag_D", [P, P])
        neg_a = sb("neg_a", [P, BLOCKS])
        w_pre = sb("w_pre", [P, P])
        b_pre = sb("b_pre", [P, 1])
        wtmp = sb("wtmp", [P, 2, HID])
        wq = sb("wq", [P, 2, HID])
        wsum = sb("wsum", [P, 2])
        wscale = sb("wscale", [P, 4])
        w1g = sb("w1g", [P, HID])
        bias1 = sb("bias1", [P, HC])
        w2g = sb("w2g", [P, HC, P])
        w2c = sb("w2c", [P, HC, P])
        lb2m = sb("lb2m", [P, HC, P])
        const_row = sb("const_row", [P, P])

        def col(name):
            a, n = COLS[name]
            return consts[:, a:a + n]

        xf = sb("xf", [P, 2, TT, P])
        xb = sb("xb", [P, 2, TT, P])
        stats_f = sb("stats_f", [P, TT, 6])
        mom_f = sb("mom_f", [P, 7, TT])
        rstd_f = sb("rstd_f", [P, TT])
        z = sb("z", [P, TT, P])
        zT = sb("zT", [P, 2, NB, SEQ + 2])
        u = sb("u", [P, CHUNK])
        B_rep = sb("B_rep", [P, 2, CHUNK])
        C_rep = sb("C_rep", [P, 2, CHUNK])
        relu_pre = sb("relu_pre", [P, CHUNK])
        abs_pre = sb("abs_pre", [P, CHUNK])
        exp_pre = sb("exp_pre", [P, CHUNK])
        ln_pre = sb("ln_pre", [P, CHUNK])
        drive_in = sb("drive_in", [P, 2, CHUNK])
        rest = sb("rest", [P, 2, CHUNK])
        parts = sb("parts", [P, PARTS, 2, CHUNK], BF16)
        stacked = sb("stacked", [P, 2, QUAD, 2, CHUNK], BF16)
        driven = sb("driven", [P, 4, CHUNK])
        state = sb("state", [P, 4, 2, CHUNK])
        gated = sb("gated", [P, 4, QUAD, CHUNK])
        y_sb = sb("y_sb", [P, CHUNK])
        stats_b = sb("stats_b", [P, TT, 6])
        mom_b = sb("mom_b", [P, 7, TT])
        rstd_b = sb("rstd_b", [P, TT])
        zz = sb("zz", [P, TT, P])
        zzT = sb("zzT", [P, CHUNK])
        x2c = sb("x2c", [P, TT, P])
        hid = sb("hid", [P, HC, CHUNK])
        hid_sq = sb("hid_sq", [P, HC, CHUNK])
        ffnT = sb("ffnT", [P, CHUNK])
        sums = sb("sums", [P, CHUNK])
        mom_t = sb("mom_t", [P, 4, TT])
        rstd_t = sb("rstd_t", [P, TT])
        ob = sb("ob", [P, 2, TT, P])

        decay = [pb(f"decay{n}") for n in range(DECAY_BANKS)]
        inflow = [pb(f"inflow{n}") for n in range(2)]
        y_ps = pb("y_ps")
        side = [pb("side0"), pb("side1")]

        s_consts = sem("consts_loaded")
        s_pool = sem("pool_setup")
        s_dve = sem("dve_setup")
        s_pe = sem("pe_setup")
        s_act = sem("act_setup")
        s_xf = [sem("xf_loaded0"), sem("xf_loaded1")]
        s_xb = [sem("xb_loaded0"), sem("xb_loaded1")]
        s_out = [sem("out_stored0"), sem("out_stored1")]
        s_stack = [sem("stacked0"), sem("stacked1")]
        s_fstat, s_frstd, s_z = sem("front_stats"), sem("front_rstd"), sem("z_ready")
        s_ztps, s_zt, s_conv, s_u = sem("zT_psum"), sem("zT_ready"), sem("conv_psum"), sem("u_ready")
        s_preps, s_bps, s_cps = sem("pre_psum"), sem("B_psum"), sem("C_psum")
        s_abs, s_exp, s_ln = sem("abs_ready"), sem("exp_ready"), sem("ln_ready")
        s_b, s_c = sem("B_ready"), sem("C_ready")
        s_dt, s_dtx = sem("dt_ready"), sem("dtx_ready")
        s_hi, s_mid, s_rest, s_lo = sem("hi_ready"), sem("mid_ready"), sem("rest_ready"), sem("lo_ready")
        s_dps, s_ips = sem("dt_spread"), sem("dtx_spread")
        s_decay, s_driven, s_state = sem("decay_ready"), sem("driven_ready"), sem("state_ready")
        s_gated, s_sum, s_skip = sem("gated_ready"), sem("quad_summed"), sem("skip_term")
        s_y, s_ytps, s_x2 = sem("y_ready"), sem("yT_psum"), sem("x2_ready")
        s_bstat, s_brstd, s_zz = sem("back_stats"), sem("back_rstd"), sem("zz_ready")
        s_zztps, s_zzt = sem("zzT_psum"), sem("zzT_ready")
        s_h1, s_gelu, s_sq = sem("hidden_psum"), sem("gelu_ready"), sem("square_ready")
        s_x2c, s_h2, s_h2c = sem("x2_const_ready"), sem("ffnT_psum"), sem("ffnT_ready")
        s_sums, s_sumsc, s_means, s_otps = sem("sums_psum"), sem("sums_ready"), sem("means_psum"), sem("ffn_psum")
        s_tstat, s_trstd, s_res = sem("tail_stats"), sem("tail_rstd"), sem("result_ready")

        x_v = x.rearrange("(c n p) d -> c p n d", n=TT, p=P)
        out_v = out.rearrange("(c n p) d -> c p n d", n=TT, p=P)
        LAST = n_chunks - 1

        def chunk(view, item):
            if item.i is None:
                return view[item.base]
            return view[bass.ds(item.times(1, 0), 1)].rearrange("c p n d -> p (c n) d")

        def live(s, stage):
            return s.i is not None or 0 <= s.base + stage <= LAST

        NORM, FRONT, COEF, SCAN, BACK, TAIL = 3, 2, 1, 0, -1, -2

        def steps(eng, setup_rest, step):
            for s in (-3, -2, -1):
                step(Item(s))
            setup_rest()
            for s in (0, 1):
                step(Item(s))
            with eng.Fori(0, (n_chunks - 6) // 2) as i:
                for par in (0, 1):
                    step(Item(2 + par, i))
            for s in range(n_chunks - 4, n_chunks + 2):
                step(Item(s))

        block = ctx.enter_context(nc.Block())

        @block.sync
        def _(sp):
            for q in (0, 1):
                sp.sem_inc(s_out[q], 16)

            def load_front(h):
                q = h.base % 2
                wait(sp, s_z, h.times(1, -1))
                sp.dma_start(xf[:, q], chunk(x_v, h)).then_inc(s_xf[q], 16)

            sp.dma_start(consts[:, :], cols).then_inc(s_consts, 16)
            sp.dma_start(dtw[:, :], dt_rows).then_inc(s_consts, 16)
            sp.dma_start(b2r[:, :], b2_row).then_inc(s_consts, 16)

            def step(s):
                q = s.base % 2
                if live(s, NORM):
                    load_front(s + NORM)
                if live(s, SCAN):
                    h = s
                    wait(sp, s_x2c, h.times(1, -1))
                    wait(sp, s_zz, h.times(1, -1))
                    sp.dma_start(xb[:, q], chunk(x_v, h)).then_inc(s_xb[q], 16)
                if live(s, COEF):
                    h = s + 1
                    qh = h.base % 2
                    wait(sp, s_ips, h.times(BLOCKS, -BLOCKS))
                    for part, ready in enumerate((s_hi, s_mid, s_lo)):
                        wait(sp, ready, h.times(1, 1))
                        for j in range(QUAD):
                            sp.dma_start(stacked[32 * part:32 * part + 32, qh, j],
                                         parts[32 * j:32 * j + 32, part]).then_inc(s_stack[qh], 16)
                if live(s, TAIL):
                    h = s + TAIL
                    wait(sp, s_res, h.times(1, 1))
                    sp.dma_start(chunk(out_v, h), ob[:, h.base % 2]).then_inc(s_out[h.base % 2], 16)

            steps(sp, lambda: None, step)
            for q in (0, 1):
                sp.wait_ge(s_out[q], 16 + 16 * (n_chunks // 2))

        @block.gpsimd
        def _(pool):
            g = nc.gpsimd
            g.memset(ident[:, :], 0.0)
            g.memset(spread[:, :, :], 0.0)
            g.memset(gather[:, :, :], 0.0)
            g.memset(ones[:, :], 1.0)
            g.memset(minus_half[:, :], -0.5)
            g.memset(pick_sum[:, :, :], 0.0)
            g.memset(avg[:, :], 1.0 / HID).then_inc(s_pool, 1)
            pool.wait_ge(s_pool, 1)
            for n in range(2):
                g.memset(pick_sum[:, n, 16 * n:16 * n + 16], 1.0)
            g.affine_select(out=ident[:, :], in_=ident[:, :], compare_op=ALU.not_equal, fill=1.0,
                            base=0, pattern=[[-1, P]], channel_multiplier=1).then_inc(s_pool, 1)
            v = spread[0:96, :, :].rearrange("p i (n c) -> p i n c", c=DSUB)
            for part in range(PARTS):
                g.affine_select(out=v, in_=v, compare_op=ALU.not_equal, fill=1.0, base=-32 * part,
                                pattern=[[-DSUB, ROUNDS_I], [0, NSTATE], [-1, DSUB]],
                                channel_multiplier=1).then_inc(s_pool, 1)
                pool.wait_ge(s_pool, 3 + part)
            flat = gather[:, :, :].rearrange("p i d -> p (i d)")
            for n in range(NSTATE):
                for i in range(ROUNDS_I):
                    a = 32 * i + DSUB * i
                    w = flat[:, a:a + DSUB]
                    last = g.affine_select(out=w, in_=w, compare_op=ALU.not_equal, fill=1.0,
                                           base=-DSUB * n, pattern=[[-1, DSUB]], channel_multiplier=1)
                last.then_inc(s_pool, 1)
                pool.wait_ge(s_pool, 3 + PARTS + n)

            def step(s):
                q = s.base % 2
                h_n, h_c, h_b, h_t = s + NORM, s + COEF, s + BACK, s + TAIL

                def rstd_norm():
                    wait(pool, s_fstat, h_n.times(5, 5))
                    wait(pool, s_z, h_n.times(1, 0))
                    g.tensor_tensor(rstd_f[:, :], mom_f[:, 6], minus_half[:, :], ALU.pow).then_inc(s_frstd, 1)

                def rstd_back():
                    wait(pool, s_bstat, h_b.times(5, 5))
                    wait(pool, s_zz, h_b.times(1, 0))
                    g.tensor_tensor(rstd_b[:, :], mom_b[:, 6], minus_half[:, :], ALU.pow).then_inc(s_brstd, 1)

                def rstd_tail():
                    wait(pool, s_tstat, h_t.times(4, 4))
                    wait(pool, s_res, h_t.times(1, 0))
                    g.tensor_tensor(rstd_t[:, :], mom_t[:, 3], minus_half[:, :], ALU.pow).then_inc(s_trstd, 1)

                def residue():
                    wait(pool, s_hi, h_c.times(1, 1))
                    g.tensor_tensor(rest[:, :, :], drive_in[:, :, :], parts[:, 0], ALU.subtract).then_inc(s_rest, 1)

                def low_part():
                    wait(pool, s_mid, h_c.times(1, 1))
                    g.tensor_tensor(parts[:, 2], rest[:, :, :], parts[:, 1], ALU.subtract).then_inc(s_lo, 1)

                for pair in range(PAIRS):
                    if live(s, SCAN):
                        wait(pool, s_state, s.times(BLOCKS, 2 * pair + 2))
                        if pair % 2 == 0:
                            wait(pool, s_sum, s.times(ROUNDS_I, pair // 2 + 1 - 4))
                        if pair == 0:
                            wait(pool, s_c, s.times(1, 1))
                        g.tensor_tensor(
                            gated[:, pair // 2, 2 * (pair % 2):2 * (pair % 2) + 2, :],
                            state[:, pair % 4, :, :],
                            C_rep[:, q, :].unsqueeze(1).broadcast_to([P, 2, CHUNK]),
                            ALU.mult).then_inc(s_gated, 1)
                    if pair == 3 and live(s, COEF):
                        residue()
                    if pair == 3 and live(s, BACK):
                        rstd_back()
                    if pair == 4 and live(s, COEF):
                        low_part()
                    if pair == 5 and live(s, TAIL):
                        rstd_tail()
                    if pair == 6 and live(s, NORM):
                        rstd_norm()
                    if pair == 7 and live(s, BACK):
                        wait(pool, s_res, h_b.times(1, 0))
                        wait(pool, s_x2, h_b.times(1, 1))
                        g.tensor_tensor(x2c[:, :, :], xb[:, h_b.base % 2],
                                        const_row[:, :].unsqueeze(1).broadcast_to([P, TT, P]),
                                        ALU.add).then_inc(s_x2c, 1)

            steps(pool, lambda: pool.wait_ge(s_dve, SETUP_DVE), step)

        @block.scalar
        def _(act):
            a = nc.scalar
            EXP_LN = "natural_log_exp_and_others"
            act.preload_act_table_set(EXP_LN)
            act.wait_ge(s_consts, 48)
            a.activation(neg_a[:, :], col("Alog"), ACT.Exp).then_inc(s_act, 1)
            act.wait_ge(s_act, 1)
            a.activation(neg_a[:, :], neg_a[:, :], ACT.Copy, scale=-1.0).then_inc(s_act, 1)
            act.wait_ge(s_act, 2)

            def step(s):
                q = s.base % 2
                h_f, h_c, h_b, h_t = s + FRONT, s + COEF, s + BACK, s + TAIL
                qf, qc = h_f.base % 2, h_c.base % 2

                def exp_block(k):
                    wait(act, s_dps, s.times(BLOCKS, k + 1))
                    v = decay[decay_bank(k)][:, :].rearrange("p (b t) -> p b t", b=NB)[:, :, 1:]
                    a.activation(v, v, ACT.Exp, scale=neg_a[:, k:k + 1]).then_inc(s_decay, 1)

                def pre_parts():
                    wait(act, s_preps, h_c.times(1, 1))
                    wait(act, s_dt, h_c.times(1, 0))
                    a.activation(relu_pre[:, :], side[0][:, :], ACT.Relu, bias=b_pre[:, 0:1])
                    a.activation(abs_pre[:, :], side[0][:, :], ACT.Abs, bias=b_pre[:, 0:1]).then_inc(s_abs, 1)

                def pre_exp():
                    wait(act, s_abs, h_c.times(1, 1))
                    a.activation(exp_pre[:, :], abs_pre[:, :], ACT.Exp, scale=-1.0).then_inc(s_exp, 1)

                def pre_ln():
                    wait(act, s_exp, h_c.times(1, 1))
                    a.activation(ln_pre[:, :], exp_pre[:, :], ACT.Ln, bias=1.0).then_inc(s_ln, 1)

                def copy_B():
                    wait(act, s_bps, h_c.times(1, 1))
                    wait(act, s_driven, h_c.times(BLOCKS, -BLOCKS))
                    a.activation(B_rep[:, qc], side[1][:, :], ACT.Identity, bias=col("bB")).then_inc(s_b, 1)

                def copy_C():
                    wait(act, s_cps, h_c.times(1, 1))
                    wait(act, s_gated, h_c.times(PAIRS, -PAIRS))
                    a.activation(C_rep[:, qc], side[0][:, :], ACT.Identity, bias=col("bC")).then_inc(s_c, 1)

                def hi_part():
                    wait(act, s_dtx, h_c.times(1, 1))
                    if h_c.i is not None or h_c.base > 0:
                        wait(act, s_stack[1 - qc], (h_c + -1).halves(16 * 12, 16 * 12))
                    a.copy(parts[:, 0], drive_in[:, :, :]).then_inc(s_hi, 1)

                def mid_part():
                    wait(act, s_rest, h_c.times(1, 1))
                    a.copy(parts[:, 1], rest[:, :, :]).then_inc(s_mid, 1)

                def copy_y():
                    wait(act, s_sum, h_b.times(ROUNDS_I, ROUNDS_I))
                    wait(act, s_ytps, h_b.times(1, 0))
                    a.copy(y_sb[:, :], y_ps[:, :]).then_inc(s_y, 1)

                def copy_zT():
                    wait(act, s_ztps, h_f.times(1, 1))
                    wait(act, s_skip, h_f.times(1, -1))
                    wait(act, s_dtx, h_f.times(1, -1))
                    a.copy(zT[:, qf, :, 1:SEQ + 1],
                           side[0][:, :].rearrange("p (b t) -> p b t", b=NB)).then_inc(s_zt, 1)

                def copy_zzT():
                    wait(act, s_zztps, h_b.times(1, 1))
                    wait(act, s_h1, h_b.times(HC, 0))
                    a.copy(zzT[:, :], side[1][:, :]).then_inc(s_zzt, 1)

                def silu():
                    wait(act, s_conv, h_f.times(1, 1))
                    wait(act, s_cps, h_f.times(1, 0))
                    a.activation(u[:, :], side[0][:, :], ACT.Silu).then_inc(s_u, 1)

                def gelu(c):
                    wait(act, s_h1, h_b.times(HC, c + 1))
                    if c == 0:
                        wait(act, s_sums, h_b.times(1, 0))
                    a.activation(hid[:, c], side[(c + 1) % 2][:, :], ACT.Gelu,
                                 bias=bias1[:, c:c + 1]).then_inc(s_gelu, 1)

                def square(n):
                    wait(act, s_gelu, h_t.times(HC, 2 * n + 2))
                    a.activation(hid_sq[:, 2 * n:2 * n + 2], hid[:, 2 * n:2 * n + 2],
                                 ACT.Square).then_inc(s_sq, 1)

                def copy_ffnT():
                    wait(act, s_h2, h_t.times(1, 1))
                    wait(act, s_otps, h_t.times(1, 0))
                    a.copy(ffnT[:, :], side[1][:, :]).then_inc(s_h2c, 1)

                def copy_sums():
                    wait(act, s_sums, h_t.times(1, 1))
                    wait(act, s_means, h_t.times(1, 0))
                    a.copy(sums[:, :], side[1][:, :]).then_inc(s_sumsc, 1)

                for k in range(BLOCKS):
                    if live(s, SCAN):
                        exp_block(k)
                    if live(s, TAIL) and k in (1, 2):
                        square(k - 1)
                    if live(s, COEF):
                        if k == 3:
                            pre_parts()
                        if k == 4:
                            pre_exp()
                            copy_B()
                        if k == 5:
                            pre_ln()
                            copy_C()
                        if k == 7:
                            hi_part()
                        if k == 10:
                            mid_part()
                    if k == 5 and live(s, BACK):
                        copy_y()
                    if k == 7 and live(s, TAIL):
                        copy_ffnT()
                    if k == 9 and live(s, TAIL):
                        copy_sums()
                    if k == 12 and live(s, FRONT):
                        copy_zT()
                    if k == 15:
                        if live(s, BACK):
                            copy_zzT()
                        if live(s, FRONT):
                            silu()
                        if live(s, BACK):
                            for c in range(HC):
                                gelu(c)
                        if live(s, FRONT) or live(s, BACK):
                            act.preload_act_table_set(EXP_LN)

            def rest_of_setup():
                act.wait_ge(s_dve, SETUP_DVE)

            act.wait_ge(s_dve, SETUP_FIRST)
            steps(act, rest_of_setup, step)

        @block.vector
        def _(dve):
            v = nc.vector
            done = [0]

            def link(ins):
                done[0] += 1
                ins.then_inc(s_dve, 1)
                dve.wait_ge(s_dve, done[0])

            for n in range(DECAY_BANKS):
                v.memset(decay[n][:, :], 0.0)
            link(v.memset(zT[:, :, :, :], 0.0))
            dve.wait_ge(s_consts, 48)
            dve.wait_ge(s_pool, 2)
            for n in range(3):
                link(v.tensor_scalar(diag_conv[:, n], ident[:, :], col("conv")[:, n:n + 1], None, ALU.mult))
            link(v.tensor_scalar(diag_D[:, :], ident[:, :], col("D"), None, ALU.mult))
            dve.wait_ge(s_pe, 1)
            link(v.tensor_copy(w_pre[:, :], y_ps[:, 0:P]))
            link(v.tensor_tensor(b_pre[:, :], y_ps[:, P:P + 1], col("bdtp"), ALU.add))
            link(v.reduce_sum(pick_row[:, 1:2],
                              ident[:, :].rearrange("p (c r) -> p c r", r=32)[:, :, 16:32], AX.XY))
            link(v.tensor_scalar(pick_row[:, 0:1], pick_row[:, 1:2], -1.0 / (16 * HID), 1.0 / (16 * HID),
                                 ALU.mult, ALU.add))
            assert done[0] == SETUP_FIRST

            def rest_of_setup():
                w_raw = consts[:, COLS["w1T"][0]:COLS["w1T"][0] + 2 * HID].rearrange("p (a n) -> p a n", a=2)
                link(v.scalar_tensor_tensor(wtmp[:, :, :], w_raw, -1.0, w_raw, ALU.mult, ALU.max))
                link(v.reduce_sum(wsum[:, :], wtmp[:, :, :], AX.X))
                dve.wait_ge(s_pe, 2)
                link(v.tensor_scalar(wscale[:, 0:2], y_ps[:, 0:2], 1.0 / (HID * P), 1e-5, ALU.mult, ALU.max))
                link(v.reciprocal(wscale[:, 2:4], wscale[:, 0:2]))
                link(v.reciprocal(wscale[:, 0:2], wscale[:, 2:4]))
                v.tensor_scalar(pick_row[:, 1:2], pick_row[:, 1:2], 1.0 / (16 * HID), None, ALU.mult)
                for m in range(2):
                    last = v.tensor_scalar(wtmp[:, m], w_raw[:, m], wscale[:, 2 + m:3 + m], 1.0, ALU.mult, ALU.min)
                link(last)
                link(v.tensor_scalar(wq[:, :, :], wtmp[:, :, :], -1.0, RINT, ALU.max, ALU.add))
                link(v.tensor_scalar(wtmp[:, :, :], wq[:, :, :], RINT, None, ALU.subtract))
                for m in range(2):
                    last = v.scalar_tensor_tensor(wq[:, m], wtmp[:, m], wscale[:, m:m + 1], w_raw[:, m],
                                                  ALU.mult, ALU.subtract)
                link(last)
                link(v.tensor_tensor(wq[:, :, :], wq[:, :, :], w_raw, ALU.add))
                link(v.tensor_scalar(w1g[:, :], wq[:, 0], col("g1"), None, ALU.mult))
                for c in range(HC):
                    v.tensor_scalar(w2g[:, c], wq[:, 1, c * P:(c + 1) * P], col("g2")[:, c:c + 1], None, ALU.mult)
                    last = v.tensor_scalar(lb2m[:, c], ones[:, :], col("lb2")[:, c:c + 1], None, ALU.mult)
                link(last)
                dve.wait_ge(s_pe, 3)
                link(v.tensor_tensor(bias1[:, :], y_ps[:, 4:4 + HC], col("b1"), ALU.add))
                link(v.tensor_copy(const_row[:, :], y_ps[:, 2 * P:3 * P]))
                for c in range(HC):
                    last = v.tensor_tensor(w2c[:, c], w2g[:, c], y_ps[:, P:2 * P], ALU.subtract)
                link(last)
                assert done[0] == SETUP_DVE, done

            def step(s):
                q = s.base % 2
                h_n, h_c, h_b, h_t = s + NORM, s + COEF, s + BACK, s + TAIL
                qn, qc, qb, qt = (h.base % 2 for h in (h_n, h_c, h_b, h_t))

                def drive_block(m, k):
                    wait(dve, s_ips, m.times(BLOCKS, k + 1))
                    if k == 0:
                        wait(dve, s_b, m.times(1, 1))
                    v.tensor_tensor(driven[:, k % 4], inflow[k % 2][:, :], B_rep[:, m.base % 2],
                                    ALU.mult).then_inc(s_driven, 1)

                def scan_block(k):
                    wait(dve, s_decay, s.times(BLOCKS, k + 1))
                    wait(dve, s_driven, s.times(BLOCKS, k + 1))
                    if k % 2 == 0:
                        wait(dve, s_gated, s.times(PAIRS, k // 2 + 1 - 4))
                    v.tensor_tensor_scan(state[:, (k // 2) % 4, k % 2], decay[decay_bank(k)][:, :],
                                         driven[:, k % 4], 0.0, ALU.mult, ALU.add).then_inc(s_state, 1)

                def moments(stats, m, done, h, scale, plus, per=5):
                    wait(dve, done, h.times(per, 1))
                    v.tensor_tensor(m[:, 0], stats[:, :, 1], stats[:, :, 4], ALU.add)
                    v.tensor_tensor(m[:, 1], stats[:, :, 1], stats[:, :, 4], ALU.subtract)
                    v.tensor_tensor(m[:, 2], stats[:, :, 2], stats[:, :, 5], ALU.add).then_inc(done, 1)
                    wait(dve, done, h.times(per, 2))
                    v.tensor_scalar(m[:, 4], m[:, 0], 0.5, None, ALU.mult)
                    v.scalar_tensor_tensor(m[:, 3], m[:, 1], 0.25, m[:, 1], ALU.mult, ALU.mult).then_inc(done, 1)
                    wait(dve, done, h.times(per, 3))
                    v.scalar_tensor_tensor(m[:, 5], m[:, 2], 1.0 / P, m[:, 3], ALU.mult, ALU.add).then_inc(done, 1)
                    wait(dve, done, h.times(per, 4))
                    v.tensor_scalar(m[:, 6], m[:, 5], scale, plus, ALU.mult, ALU.add).then_inc(done, 1)

                def norm_stats():
                    wait(dve, s_xf[qn], h_n.halves(16, 16))
                    for n in range(TT):
                        last = v.bn_stats(stats_f[:, n], xf[:, qn, n])
                    last.then_inc(s_fstat, 1)
                    moments(stats_f, mom_f, s_fstat, h_n, 1.0, EPS)

                def norm_z():
                    wait(dve, s_frstd, h_n.times(1, 1))
                    wait(dve, s_ztps, h_n.times(1, 0))
                    for n in range(TT):
                        last = v.tensor_scalar(z[:, n], xf[:, qn, n], mom_f[:, 4, n:n + 1], rstd_f[:, n:n + 1],
                                               ALU.subtract, ALU.mult)
                    last.then_inc(s_z, 1)

                def dt_parts():
                    wait(dve, s_ln, h_c.times(1, 1))
                    wait(dve, s_rest, h_c.times(1, 0))
                    wait(dve, s_zt, h_c.times(1, 1))
                    v.tensor_tensor(drive_in[:, 0], relu_pre[:, :], ln_pre[:, :], ALU.add).then_inc(s_dt, 1)
                    wait(dve, s_dt, h_c.times(1, 1))
                    v.tensor_tensor(drive_in[:, 1].rearrange("p (b t) -> p b t", b=NB),
                                    drive_in[:, 0].rearrange("p (b t) -> p b t", b=NB),
                                    zT[:, qc, :, 1:SEQ + 1], ALU.mult).then_inc(s_dtx, 1)

                def back_residual():
                    wait(dve, s_ytps, h_b.times(1, 1))
                    wait(dve, s_xb[qb], h_b.halves(16, 16))
                    v.tensor_tensor(xb[:, qb], xb[:, qb],
                                    side[0][:, :].rearrange("p (n d) -> p n d", n=TT),
                                    ALU.add).then_inc(s_x2, 1)
                    wait(dve, s_x2, h_b.times(1, 1))
                    for n in range(TT):
                        last = v.bn_stats(stats_b[:, n], xb[:, qb, n])
                    last.then_inc(s_bstat, 1)
                    moments(stats_b, mom_b, s_bstat, h_b, 1.0 + EPS, EPS * EPS)

                def back_zz():
                    wait(dve, s_brstd, h_b.times(1, 1))
                    wait(dve, s_zztps, h_b.times(1, 0))
                    for n in range(TT):
                        last = v.tensor_scalar(zz[:, n], xb[:, qb, n], mom_b[:, 4, n:n + 1], rstd_b[:, n:n + 1],
                                               ALU.subtract, ALU.mult)
                    last.then_inc(s_zz, 1)

                def tail_stats():
                    means = side[0][:, 0:2 * TT].rearrange("p (n c) -> p n c", c=2)
                    wait(dve, s_means, h_t.times(1, 1))
                    v.tensor_copy(mom_t[:, 0], means[:, :, 0]).then_inc(s_tstat, 1)
                    wait(dve, s_tstat, h_t.times(4, 1))
                    v.tensor_tensor(mom_t[:, 1], mom_t[:, 0], mom_t[:, 0], ALU.mult).then_inc(s_tstat, 1)
                    wait(dve, s_tstat, h_t.times(4, 2))
                    v.tensor_tensor(mom_t[:, 2], means[:, :, 1], mom_t[:, 1], ALU.subtract).then_inc(s_tstat, 1)
                    wait(dve, s_tstat, h_t.times(4, 3))
                    v.tensor_scalar(mom_t[:, 3], mom_t[:, 2], 0.0, EPS, ALU.max, ALU.add).then_inc(s_tstat, 1)

                def tail_result():
                    wait(dve, s_x2c, h_t.times(1, 1))
                    wait(dve, s_out[qt], h_t.halves(16, 16))
                    wait(dve, s_otps, h_t.times(1, 1))
                    wait(dve, s_trstd, h_t.times(1, 1))
                    for n in range(TT):
                        last = v.scalar_tensor_tensor(ob[:, qt, n], side[1][:, n * P:(n + 1) * P],
                                                      rstd_t[:, n:n + 1], x2c[:, n], ALU.mult, ALU.add)
                    last.then_inc(s_res, 1)

                if s.i is None and s.base == 0:
                    drive_block(s, 0)
                for k in range(BLOCKS):
                    if live(s, SCAN):
                        if k < BLOCKS - 1:
                            drive_block(s, k + 1)
                        scan_block(k)
                    if k == BLOCKS - 1 and live(s, SCAN) and live(s + 1, SCAN):
                        drive_block(s + 1, 0)
                    if k == 5 and live(s, COEF):
                        dt_parts()
                    if k == 7 and live(s, BACK):
                        back_residual()
                    if k == 9 and live(s, TAIL):
                        tail_stats()
                    if k == 10 and live(s, BACK):
                        back_zz()
                    if k == 12 and live(s, TAIL):
                        tail_result()
                    if k == 13 and live(s, NORM):
                        norm_stats()
                    if k == 15 and live(s, NORM):
                        norm_z()

            steps(dve, rest_of_setup, step)

        @block.tensor
        def _(pe):
            mm = nc.tensor.matmul
            pe.wait_ge(s_consts, 48)
            mm(y_ps[:, 0:P], dtw[:, 0:P], dtw[:, P:2 * P], start=True, stop=True)
            mm(y_ps[:, P:P + 1], dtw[:, P:2 * P], dtw[:, 2 * P:2 * P + 1], start=True, stop=True).then_inc(s_pe, 1)
            pe.wait_ge(s_pool, 2 + PARTS + NSTATE)
            pe.wait_ge(s_dve, SETUP_FIRST)

            def rest_of_setup():
                pe.wait_ge(s_dve, SETUP_FIRST + 2)
                mm(y_ps[:, 0:2], ones[:, :], wsum[:, :], start=True, stop=True).then_inc(s_pe, 1)
                pe.wait_ge(s_dve, SETUP_DVE - 3)
                for c in range(HC):
                    mm(y_ps[:, 4 + c:5 + c], wq[:, 0, c * P:(c + 1) * P], col("lb1"), start=True, stop=True)
                for c in range(HC):
                    mm(y_ps[:, P:2 * P], avg[:, :], w2g[:, c], start=(c == 0), stop=(c == HC - 1))
                for c in range(HC):
                    mm(y_ps[:, 2 * P:3 * P], lb2m[:, c], wq[:, 1, c * P:(c + 1) * P], start=(c == 0), stop=False)
                mm(y_ps[:, 2 * P:3 * P], ones[0:1, :], b2r[:, :], start=False, stop=True).then_inc(s_pe, 1)
                pe.wait_ge(s_dve, SETUP_DVE)

            def step(s):
                q = s.base % 2
                h_f, h_c, h_b, h_t = s + FRONT, s + COEF, s + BACK, s + TAIL
                qf = h_f.base % 2

                def spread_block(k):
                    i, j = k // QUAD, k % QUAD
                    if k == 0:
                        wait(pe, s_stack[q], s.halves(16 * 12, 16 * 12))
                    wait(pe, s_state, s.times(BLOCKS, k + 1 - decay_before(k)))
                    mm(decay[decay_bank(k)][:, :].rearrange("p (b t) -> p b t", b=NB)[:, :, 1:],
                       spread[0:96, i], stacked[0:96, q, j, 0].rearrange("p (b t) -> p b t", b=NB)[:, :, 1:],
                       start=True, stop=True).then_inc(s_dps, 1)
                    wait(pe, s_driven, s.times(BLOCKS, k + 1 - 2))
                    mm(inflow[k % 2][:, :], spread[0:96, i], stacked[0:96, q, j, 1],
                       start=True, stop=True).then_inc(s_ips, 1)

                def sum_quad(m, i):
                    wait(pe, s_gated, m.times(PAIRS, 2 * i + 2))
                    for j in range(QUAD):
                        last = mm(y_ps[32 * j:32 * j + 32, :], gather[:, i], gated[:, i, j],
                                  start=False, stop=(i == ROUNDS_I - 1), skip_group_check=True)
                    last.then_inc(s_sum, 1)

                def skip_term():
                    wait(pe, s_y, s.times(1, 0))
                    mm(y_ps[:, :].rearrange("p (b t) -> p b t", b=NB), diag_D[:, :], zT[:, q, :, 1:SEQ + 1],
                       start=True, stop=False, skip_group_check=True).then_inc(s_skip, 1)

                def pre():
                    wait(pe, s_u, h_c.times(1, 1))
                    wait(pe, s_gelu, h_c.times(HC, -3 * HC + 4))
                    mm(side[0][:, :], w_pre[:, :], u[:, :], start=True, stop=True).then_inc(s_preps, 1)

                def fill_B():
                    wait(pe, s_gelu, h_c.times(HC, -3 * HC + 3))
                    mm(side[1][:, :], col("wB"), u[:, :], start=True, stop=True).then_inc(s_bps, 1)

                def fill_C():
                    wait(pe, s_abs, h_c.times(1, 1))
                    mm(side[0][:, :], col("wC"), u[:, :], start=True, stop=True).then_inc(s_cps, 1)

                def second(half):
                    if half == 0:
                        wait(pe, s_gelu, h_t.times(HC, HC))
                        if live(s, COEF):
                            wait(pe, s_b, h_c.times(1, 1))
                    for c in (2 * half, 2 * half + 1):
                        last = mm(side[1][:, :], w2c[:, c], hid[:, c], start=(c == 0), stop=(c == HC - 1))
                    if half == 1:
                        last.then_inc(s_h2, 1)

                def transpose_y():
                    wait(pe, s_y, h_b.times(1, 1))
                    if live(s, COEF):
                        wait(pe, s_c, h_c.times(1, 1))
                    for n in range(TT):
                        last = nc.tensor.transpose(side[0][:, n * P:(n + 1) * P], y_sb[:, n * P:(n + 1) * P], ident[:, :])
                    last.then_inc(s_ytps, 1)

                def hidden_sums():
                    wait(pe, s_sq, h_t.times(2, 2))
                    wait(pe, s_h2c, h_t.times(1, 1))
                    for n, src in enumerate((hid, hid_sq)):
                        for c in range(HC):
                            last = mm(side[1][32 * c:32 * c + 32, :], pick_sum[:, n], src[:, c],
                                      start=(n == 0), stop=(n == 1), skip_group_check=True)
                    last.then_inc(s_sums, 1)

                def hidden_means():
                    wait(pe, s_sumsc, h_t.times(1, 1))
                    if live(s, BACK):
                        wait(pe, s_x2, h_b.times(1, 1))
                    for n in range(TT):
                        last = mm(side[0][:, 2 * n:2 * n + 2], sums[:, n * P:(n + 1) * P], pick_row[:, :],
                                  start=True, stop=True)
                    last.then_inc(s_means, 1)

                def transpose_ffn():
                    wait(pe, s_h2c, h_t.times(1, 1))
                    for n in range(TT):
                        last = nc.tensor.transpose(side[1][:, n * P:(n + 1) * P], ffnT[:, n * P:(n + 1) * P], ident[:, :])
                    last.then_inc(s_otps, 1)

                def transpose_z():
                    wait(pe, s_z, h_f.times(1, 1))
                    if live(s, TAIL):
                        wait(pe, s_tstat, h_t.times(4, 3))
                    elif live(s, BACK):
                        wait(pe, s_x2, h_b.times(1, 1))
                    elif live(s, COEF):
                        wait(pe, s_c, h_c.times(1, 1))
                    for n in range(TT):
                        last = nc.tensor.transpose(side[0][:, n * P:(n + 1) * P], z[:, n], ident[:, :])
                    last.then_inc(s_ztps, 1)

                def convolve():
                    wait(pe, s_zt, h_f.times(1, 1))
                    for n in range(3):
                        last = mm(side[0][:, :].rearrange("p (b t) -> p b t", b=NB), diag_conv[:, n],
                                  zT[:, qf, :, n:n + SEQ], start=(n == 0), stop=(n == 2))
                    last.then_inc(s_conv, 1)

                def transpose_zz():
                    wait(pe, s_zz, h_b.times(1, 1))
                    if live(s, TAIL):
                        wait(pe, s_res, h_t.times(1, 1))
                    elif live(s, COEF):
                        wait(pe, s_b, h_c.times(1, 1))
                    for n in range(TT):
                        last = nc.tensor.transpose(side[1][:, n * P:(n + 1) * P], zz[:, n], ident[:, :])
                    last.then_inc(s_zztps, 1)

                def first(h, c):
                    if c == 0:
                        wait(pe, s_zzt, h.times(1, 1))
                    elif c == 1:
                        if live(h, FRONT - BACK):
                            wait(pe, s_u, (h + (FRONT - BACK)).times(1, 1))
                        else:
                            wait(pe, s_tstat, h.times(4, 0))
                    else:
                        wait(pe, s_gelu, h.times(HC, c - 1))
                    mm(side[(c + 1) % 2][:, :], w1g[:, c * P:(c + 1) * P], zzT[:, :],
                       start=True, stop=True).then_inc(s_h1, 1)

                for k in range(BLOCKS):
                    if live(s, SCAN):
                        spread_block(k)
                    if k <= 2 and live(s, TAIL):
                        first(h_t, k + 1)
                    if live(s, COEF):
                        if k == 2:
                            pre()
                        if k == 3:
                            fill_B()
                        if k == 4:
                            fill_C()
                    if k == 3 and live(s, BACK):
                        sum_quad(h_b, 3)
                    if live(s, TAIL) and k in (5, 6):
                        second(k - 5)
                    if k == 6 and live(s, BACK):
                        transpose_y()
                    if k == 7 and live(s, SCAN):
                        skip_term()
                    if k == 8 and live(s, TAIL):
                        hidden_sums()
                    if k == 8 and live(s, SCAN):
                        sum_quad(s, 0)
                    if k == 9 and live(s, TAIL):
                        hidden_means()
                    if k == 10 and live(s, TAIL):
                        transpose_ffn()
                    if k == 11 and live(s, FRONT):
                        transpose_z()
                    if k == 12 and live(s, SCAN):
                        sum_quad(s, 1)
                    if k == 13 and live(s, FRONT):
                        convolve()
                    if k == 14 and live(s, BACK):
                        transpose_zz()
                    if k == 15 and live(s, SCAN):
                        sum_quad(s, 2)
                    if k == 15 and live(s, BACK):
                        first(h_b, 0)

            steps(pe, rest_of_setup, step)


def kernel(**inputs):
    import numpy as np
    import concourse.bacc as bacc
    from concourse.bass_utils import run_bass_kernel_spmd

    a = {k: np.asarray(v) for k, v in inputs.items()}
    f = lambda name: a["L0_" + name]
    xs = f("attn_x")
    tokens = xs.shape[0] * xs.shape[1]
    a_log = f("attn_A_log").reshape(QUAD, ROUNDS_I, DSUB, NSTATE).transpose(3, 2, 1, 0).reshape(P, BLOCKS)
    w_bc, b_bc = f("attn_W_bc"), f("attn_b_bc")
    packed = {
        "conv": f("attn_conv_w").T,
        "bB": np.repeat(b_bc[:NSTATE], DSUB)[:, None], "bC": np.repeat(b_bc[NSTATE:], DSUB)[:, None],
        "bdtp": f("attn_b_dtp")[:, None], "D": f("attn_Dcoeff")[:, None],
        "g1": f("ffn_ln1_g")[:, None], "lb1": f("ffn_ln1_b")[:, None],
        "b1": f("ffn_b1").reshape(HC, P).T, "g2": f("ffn_ln2_g").reshape(HC, P).T,
        "lb2": f("ffn_ln2_b").reshape(HC, P).T, "Alog": a_log,
        "wB": np.repeat(w_bc[:, :NSTATE], DSUB, axis=1), "wC": np.repeat(w_bc[:, NSTATE:], DSUB, axis=1),
        "w1T": f("ffn_w1").T,
        "w2T": f("ffn_w2").T.reshape(HC, P, P).transpose(1, 0, 2).reshape(P, HID),
    }
    arrays = {
        "x": np.ascontiguousarray(xs.reshape(tokens, P)),
        "cols": np.ascontiguousarray(np.concatenate([packed[k] for k in COLS], axis=1)),
        "dt_rows": np.ascontiguousarray(np.concatenate(
            [f("attn_W_dt").T, f("attn_W_dtp"), f("attn_b_dt")[:, None]], axis=1)),
        "b2_row": np.ascontiguousarray(f("ffn_b2")[None, :]),
    }
    nc = bacc.Bacc("TRN2", target_bir_lowering=False, num_devices=1)
    aps = [nc.dram_tensor(k, v.shape, mybir.dt.from_np(v.dtype), kind="ExternalInput").ap()
           for k, v in arrays.items()]
    out = nc.dram_tensor("out", (tokens, P), F32, kind="ExternalOutput").ap()
    preln_ssm_ffn(nc, *aps, out, tokens // CHUNK)
    r = run_bass_kernel_spmd(nc, [arrays], core_ids=[0])
    return r.results[0]["out"].reshape(xs.shape)
```

```python
from contextlib import ExitStack

import concourse.bass as bass
import concourse.mybir as mybir

F32 = mybir.dt.float32
BF16 = mybir.dt.bfloat16
ALU = mybir.AluOpType
ACT = mybir.ActivationFunctionType
AX = mybir.AxisListType

P = 128
SEQ = 256
NSTATE = 16
DSUB = P // NSTATE
CHUNK = 512
NB = CHUNK // SEQ
TT = CHUNK // P
QUAD = 4
BLOCKS = P // DSUB
PAIRS = BLOCKS // 2
ROUNDS_I = BLOCKS // QUAD
HID = 512
HC = HID // P
PARTS = 3
DRIVE_BANKS = 3
DECAYS = 8
DECAY_AT = (-1, -1, 0, 1, 2, 2, 3, 4, 5, 6, 7, 7, 8, 9, 10, 11)
DECAY_SLOTS = [[b for b in range(BLOCKS) if DECAY_AT[b] == k]
               + [BLOCKS + b for b in range(BLOCKS) if DECAY_AT[b] == k - BLOCKS]
               for k in range(BLOCKS)]
EPS = 1e-5
SETUP_DIAG, SETUP_PRE, SETUP_SUMS, SETUP_GAINS, SETUP_ALL = 5, 7, 9, 19, 22
HIDDEN_BANK = (2, 0, 1, 2)
PE_AT = dict(second=(1, 2, 2, 3), quad2=0, BC=2, quad3=3, sums=(4, 5), skip=6, yT=9, zT=8, quad0=7,
             sumsT=11, conv=(9, 10, 11), first=(11, 11, 12, 13), quad1=14, pre=14, zzT=15, ffn=15)
ACT_AT = dict(exp_pre=1, ln_pre=1, zzT=0, square0=2, BC=3, square1=2, hi=5, y=4, ffnT=6, sums=7,
              mid=9, zT=8, tables=11, pre=15)
DVE_AT = dict(norm_stats=0, dt_parts=1, norm_z=3, residual=8, tail_stats=9, zz=13, result=15)
POOL_AT = dict(residual_const=1, residue=1, low_part=2, rstd_back=4, rstd_tail=5)
PE_START = dict(PE_AT, BC=1, zT=11, conv=(11, 12, 12), pre=15)
ACT_START = dict(ACT_AT, BC=2, hi=2, mid=7, zT=5, tables=10)
DVE_START = dict(DVE_AT, dt_parts=2, norm_z=13)
PE_END = dict(PE_AT, second=(1, 2, 3, 5), quad2=3, quad3=4, sums=(4, 7), yT=4, sumsT=9,
              first=(8, 10, 10, 11), zzT=12, ffn=12)
ACT_END = dict(ACT_AT, zzT=6, square0=0, square1=3, y=9, ffnT=11, sums=11, tables=13)
DVE_END = dict(DVE_AT, residual=1, tail_stats=5, zz=10, result=12)
RINT = 1.5 * 2.0 ** 23

COLS = {}
_at = 0
for _name, _n in (("conv", 3), ("bBC", 1), ("bdtp", 1), ("D", 1), ("g1", 1), ("lb1", 1),
                  ("b1", HC), ("g2", HC), ("lb2", HC), ("Alog", BLOCKS),
                  ("wBC", 2 * NSTATE), ("w1T", HID), ("w2T", HID)):
    COLS[_name] = (_at, _n)
    _at += _n
NCOLS = _at
FIRST_COLS = COLS["w1T"][0]


def drive_bank(k):
    return k % DRIVE_BANKS if k < BLOCKS - 1 else 1


def drive_before(k):
    for back in range(1, BLOCKS + 1):
        if drive_bank((k - back) % BLOCKS) == drive_bank(k):
            return back


class Item:

    def __init__(self, base, i=None):
        self.base, self.i = base, i

    def __add__(self, n):
        return Item(self.base + n, self.i)

    def times(self, per, plus):
        v = per * self.base + plus
        return v if self.i is None else self.i * (2 * per) + v

    def halves(self, per, plus):
        v = per * (self.base // 2) + plus
        return v if self.i is None else self.i * per + v


def wait(eng, sem, value):
    if isinstance(value, int) and value <= 0:
        return
    eng.wait_ge(sem, value)


def preln_ssm_ffn(nc, x, cols, dt_rows, b2_row, out, n_chunks):
    ctx = ExitStack()

    def sb(name, shape, dt=F32):
        return ctx.enter_context(nc.sbuf_tensor(name, shape, dt))

    def pb(name):
        return ctx.enter_context(nc.psum_tensor(name, [P, CHUNK], F32))

    def sem(name):
        return ctx.enter_context(nc.semaphore(name))

    with ctx:
        consts = sb("consts", [P, NCOLS])
        dtw = sb("dtw", [8, 2 * P + 1])
        b2r = sb("b2r", [1, P])
        ident = sb("ident", [P, P])
        ones = sb("ones", [P, P])
        avg = sb("avg", [P, P])
        pick_sum = sb("pick_sum", [P, 2, 32])
        minus_half = sb("minus_half", [P, TT])
        spread = sb("spread", [P, ROUNDS_I, P], BF16)
        gather = sb("gather", [P, ROUNDS_I, 32])
        diag_conv = sb("diag_conv", [P, 3, P])
        diag_D = sb("diag_D", [P, P])
        neg_a = sb("neg_a", [P, BLOCKS])
        w_pre = sb("w_pre", [P, P])
        b_pre = sb("b_pre", [P, 1])
        wq = sb("wq", [P, 2, HID])
        wsum = sb("wsum", [P, 2])
        wscale = sb("wscale", [P, 4])
        w1g = sb("w1g", [P, HID])
        bias1 = sb("bias1", [P, HC])
        w2g = sb("w2g", [P, HC, P])
        w2c = sb("w2c", [P, HC, P])
        const_row = sb("const_row", [P, P])

        def col(name):
            a, n = COLS[name]
            return consts[:, a:a + n]

        xf = sb("xf", [P, 2, TT, P])
        xb = sb("xb", [P, TT, P])
        x2 = sb("x2", [P, 2, TT, P])
        stats_f = sb("stats_f", [P, TT, 6])
        mom_f = sb("mom_f", [P, 7, TT])
        rstd_f = sb("rstd_f", [P, TT])
        z = sb("z", [P, TT, P])
        zT = sb("zT", [P, 2, NB, SEQ + 2])
        u = sb("u", [P, CHUNK])
        bc = sb("bc", [2 * NSTATE, CHUNK])
        B_rep = sb("B_rep", [P, 2, CHUNK])
        C_rep = sb("C_rep", [P, 2, CHUNK])
        relu_pre = sb("relu_pre", [P, CHUNK])
        soft_pre = sb("soft_pre", [P, CHUNK])
        ln_pre = sb("ln_pre", [P, CHUNK])
        drive_in = sb("drive_in", [P, 2, CHUNK])
        rest = sb("rest", [P, 2, CHUNK])
        parts = sb("parts", [P, PARTS, 2, CHUNK], BF16)
        stacked = sb("stacked", [P, 2, QUAD, 2, CHUNK], BF16)
        decay = sb("decay", [P, DECAYS, CHUNK])
        state = sb("state", [P, 4, 2, CHUNK])
        gated = sb("gated", [P, 4, QUAD, CHUNK])
        y_sb = sb("y_sb", [P, CHUNK])
        stats_b = sb("stats_b", [P, TT, 6])
        mom_b = sb("mom_b", [P, 7, TT])
        rstd_b = sb("rstd_b", [P, TT])
        zz = sb("zz", [P, TT, P])
        zzT = sb("zzT", [P, CHUNK])
        x2c = sb("x2c", [P, TT, P])
        hid = sb("hid", [P, HC, CHUNK])
        hid_sq = sb("hid_sq", [P, HC, CHUNK])
        ffnT = sb("ffnT", [P, CHUNK])
        sums = sb("sums", [P, CHUNK])
        mom_t = sb("mom_t", [P, 5, TT])
        rstd_t = sb("rstd_t", [P, TT])
        ob = sb("ob", [P, 2, TT, P])

        wtmp = hid[:, 0:2, :]
        lb2m = hid_sq[:, 0].rearrange("p (c n) -> p c n", c=HC)

        dt_ps = pb("dt_ps")
        driven = [pb(f"driven{n}") for n in range(DRIVE_BANKS)]
        y_ps = pb("y_ps")
        side = [pb("side0"), pb("side1"), pb("side2")]

        s_consts, s_weights = sem("consts_loaded"), sem("weights_loaded")
        s_pool = sem("pool_setup")
        s_dve = sem("dve_setup")
        s_pe = sem("pe_setup")
        s_act = sem("act_setup")
        s_xf = [sem("xf_loaded0"), sem("xf_loaded1")]
        s_xb = sem("xb_loaded")
        s_out = [sem("out_stored0"), sem("out_stored1")]
        s_stack = [sem("stacked0"), sem("stacked1")]
        s_fstat, s_frstd, s_z = sem("front_stats"), sem("front_rstd"), sem("z_ready")
        s_ztps, s_zt, s_conv, s_u = sem("zT_psum"), sem("zT_ready"), sem("conv_psum"), sem("u_ready")
        s_preps, s_bcps = sem("pre_psum"), sem("BC_psum")
        s_abs, s_exp, s_ln = sem("abs_ready"), sem("exp_ready"), sem("ln_ready")
        s_bc, s_b, s_c = sem("BC_ready"), sem("B_spread"), sem("C_spread")
        s_dt, s_dtx = sem("dt_ready"), sem("dtx_ready")
        s_hi, s_mid, s_rest, s_lo = sem("hi_ready"), sem("mid_ready"), sem("rest_ready"), sem("lo_ready")
        s_dps, s_xps = sem("dt_spread"), sem("dtx_spread")
        s_decay, s_driven, s_state = sem("decay_ready"), sem("driven_ready"), sem("state_ready")
        s_gated, s_sum, s_skip = sem("gated_ready"), sem("quad_summed"), sem("skip_term")
        s_y, s_ytps, s_x2 = sem("y_ready"), sem("yT_psum"), sem("x2_ready")
        s_bstat, s_brstd, s_zz = sem("back_stats"), sem("back_rstd"), sem("zz_ready")
        s_zztps, s_zzt = sem("zzT_psum"), sem("zzT_ready")
        s_hid, s_gelu, s_sq = sem("hidden_psum"), sem("gelu_ready"), sem("square_ready")
        s_x2c, s_ffntps, s_ffnt = sem("x2_const_ready"), sem("ffnT_psum"), sem("ffnT_ready")
        s_sums, s_sumsc, s_sumst, s_ffnps = sem("sums_psum"), sem("sums_ready"), sem("sumsT_psum"), sem("ffn_psum")
        s_tstat, s_trstd, s_res = sem("tail_stats"), sem("tail_rstd"), sem("result_ready")

        x_v = x.rearrange("(c n p) d -> c p n d", n=TT, p=P)
        out_v = out.rearrange("(c n p) d -> c p n d", n=TT, p=P)
        LAST = n_chunks - 1

        def chunk(view, item):
            if item.i is None:
                return view[item.base]
            return view[bass.ds(item.times(1, 0), 1)].rearrange("c p n d -> p (c n) d")

        def live(s, stage):
            return s.i is not None or 0 <= s.base + stage <= LAST

        FRONT, COEF, SCAN, BACK, FFN, TAIL = 2, 1, 0, -1, -2, -3
        LOOP_START = 1 - TAIL

        def slots(s, start, full, end):
            if s.i is None and s.base < 0:
                return start
            return end if s.i is None and s.base > LAST else full

        def at_start(s, n):
            return s.i is None and s.base == n

        def steps(step, eng):
            for s in range(-FRONT, 0):
                step(Item(s))
            for s in range(0, LOOP_START):
                step(Item(s))
            rounds = (n_chunks - FRONT - LOOP_START) // 2
            with eng.Fori(0, rounds) as i:
                for par in (0, 1):
                    step(Item(LOOP_START + par, i))
            for s in range(LOOP_START + 2 * rounds, n_chunks - TAIL):
                step(Item(s))

        block = ctx.enter_context(nc.Block())

        @block.sync
        def _(sp):
            for q in (0, 1):
                sp.sem_inc(s_out[q], 16)

            def load_front(h):
                q = h.base % 2
                wait(sp, s_z, h.times(1, -1))
                sp.dma_start(xf[:, q], chunk(x_v, h)).then_inc(s_xf[q], 16)

            sp.dma_start(consts[:, 0:FIRST_COLS], cols[:, 0:FIRST_COLS]).then_inc(s_consts, 16)
            load_front(Item(0))
            sp.dma_start(dtw[:, :], dt_rows).then_inc(s_consts, 16)
            sp.dma_start(consts[:, FIRST_COLS:], cols[:, FIRST_COLS:]).then_inc(s_weights, 16)
            sp.dma_start(b2r[:, :], b2_row).then_inc(s_weights, 16)

            def store(h):
                wait(sp, s_res, h.times(1, 1))
                sp.dma_start(chunk(out_v, h), ob[:, h.base % 2]).then_inc(s_out[h.base % 2], 16)

            def step(s):
                h = s + COEF
                qh = h.base % 2

                def spread_states(first, to, done):
                    rows = bc[first:first + NSTATE, :].unsqueeze(1).broadcast_to([NSTATE, DSUB, CHUNK])
                    sp.dma_start(to, rows).then_inc(done, 16)

                def stack_part(part, ready):
                    wait(sp, ready, h.times(1, 1))
                    for j in range(QUAD):
                        sp.dma_start(stacked[32 * part:32 * part + 32, qh, j],
                                     parts[32 * j:32 * j + 32, part]).then_inc(s_stack[qh], 16)

                if live(s, FRONT) and not at_start(s, -FRONT):
                    load_front(s + FRONT)
                if live(s, COEF):
                    wait(sp, s_driven, h.times(BLOCKS, -BLOCKS))
                    wait(sp, s_bc, h.times(1, 1))
                    spread_states(0, B_rep[:, qh], s_b)
                    stack_part(0, s_hi)
                    wait(sp, s_gated, h.times(PAIRS, -PAIRS))
                    spread_states(NSTATE, C_rep[:, qh], s_c)
                if live(s, SCAN):
                    wait(sp, s_x2, s.times(1, 0))
                    sp.dma_start(xb[:, :, :], chunk(x_v, s)).then_inc(s_xb, 16)
                if live(s, TAIL - 1):
                    store(s + (TAIL - 1))
                if live(s, COEF):
                    stack_part(1, s_mid)
                    stack_part(2, s_lo)

            steps(step, sp)
            store(Item(LAST))
            for q in (0, 1):
                sp.wait_ge(s_out[q], 16 + 16 * (n_chunks // 2))

        @block.gpsimd
        def _(pool):
            g = nc.gpsimd
            g.memset(ident[:, :], 0.0)
            g.memset(spread[:, :, :], 0.0)
            g.memset(gather[:, :, :], 0.0)
            g.memset(ones[:, :], 1.0)
            g.memset(minus_half[:, :], -0.5)
            g.memset(pick_sum[:, :, :], 0.0)
            g.memset(avg[:, :], 1.0 / HID).then_inc(s_pool, 1)
            pool.wait_ge(s_pool, 1)
            for n in range(2):
                g.memset(pick_sum[:, n, 16 * n:16 * n + 16], 1.0)
            g.affine_select(out=ident[:, :], in_=ident[:, :], compare_op=ALU.not_equal, fill=1.0,
                            base=0, pattern=[[-1, P]], channel_multiplier=1).then_inc(s_pool, 1)

            def spread_matrix():
                v = spread[0:96, :, :].rearrange("p i (n c) -> p i n c", c=DSUB)
                for part in range(PARTS):
                    g.affine_select(out=v, in_=v, compare_op=ALU.not_equal, fill=1.0, base=-32 * part,
                                    pattern=[[-DSUB, ROUNDS_I], [0, NSTATE], [-1, DSUB]],
                                    channel_multiplier=1).then_inc(s_pool, 1)
                    pool.wait_ge(s_pool, 3 + part)

            def gather_matrix():
                flat = gather[:, :, :].rearrange("p i d -> p (i d)")
                for n in range(NSTATE):
                    for i in range(ROUNDS_I):
                        a = 32 * i + DSUB * i
                        w = flat[:, a:a + DSUB]
                        last = g.affine_select(out=w, in_=w, compare_op=ALU.not_equal, fill=1.0,
                                               base=-DSUB * n, pattern=[[-1, DSUB]], channel_multiplier=1)
                    last.then_inc(s_pool, 1)
                    pool.wait_ge(s_pool, 3 + PARTS + n)

            def step(s):
                q = s.base % 2
                h_n, h_c, h_b, h_t = s + FRONT, s + COEF, s + BACK, s + TAIL
                qt = h_t.base % 2

                def rstd_norm():
                    wait(pool, s_fstat, h_n.times(4, 4))
                    wait(pool, s_z, h_n.times(1, 0))
                    g.tensor_tensor(rstd_f[:, :], mom_f[:, 6], minus_half[:, :], ALU.pow).then_inc(s_frstd, 1)

                def rstd_back():
                    wait(pool, s_bstat, h_b.times(4, 4))
                    wait(pool, s_zz, h_b.times(1, 0))
                    g.tensor_tensor(rstd_b[:, :], mom_b[:, 6], minus_half[:, :], ALU.pow).then_inc(s_brstd, 1)

                def rstd_tail():
                    wait(pool, s_tstat, h_t.times(4, 4))
                    wait(pool, s_res, h_t.times(1, 0))
                    g.tensor_tensor(rstd_t[:, :], mom_t[:, 4], minus_half[:, :], ALU.pow).then_inc(s_trstd, 1)

                def residue():
                    wait(pool, s_hi, h_c.times(1, 1))
                    wait(pool, s_lo, h_c.times(1, 0))
                    g.tensor_tensor(rest[:, :, :], drive_in[:, :, :], parts[:, 0], ALU.subtract).then_inc(s_rest, 1)

                def low_part():
                    wait(pool, s_rest, h_c.times(1, 1))
                    wait(pool, s_mid, h_c.times(1, 1))
                    g.tensor_tensor(parts[:, 2], rest[:, :, :], parts[:, 1], ALU.subtract).then_inc(s_lo, 1)

                def residual_const():
                    wait(pool, s_res, h_t.times(1, 0))
                    wait(pool, s_x2, h_t.times(1, 1))
                    g.tensor_tensor(x2c[:, :, :], x2[:, qt],
                                    const_row[:, :].unsqueeze(1).broadcast_to([P, TT, P]),
                                    ALU.add).then_inc(s_x2c, 1)

                if live(s, FRONT):
                    rstd_norm()
                if at_start(s, -FRONT):
                    spread_matrix()
                if at_start(s, 0):
                    pool.wait_ge(s_dve, SETUP_ALL)
                at = POOL_AT
                for pair in range(PAIRS):
                    if live(s, SCAN):
                        wait(pool, s_state, s.times(BLOCKS, 2 * pair + 2))
                        if pair % 2 == 0:
                            wait(pool, s_sum, s.times(ROUNDS_I, pair // 2 + 1 - 4))
                        if pair == 0:
                            wait(pool, s_c, s.times(16, 16))
                        g.tensor_tensor(
                            gated[:, pair // 2, 2 * (pair % 2):2 * (pair % 2) + 2, :],
                            state[:, pair % 4, :, :],
                            C_rep[:, q, :].unsqueeze(1).broadcast_to([P, 2, CHUNK]),
                            ALU.mult).then_inc(s_gated, 1)
                    if pair == at["residual_const"] and live(s, TAIL):
                        residual_const()
                    if pair == at["residue"] and live(s, COEF):
                        residue()
                    if pair == at["low_part"] and live(s, COEF):
                        low_part()
                    if pair == at["low_part"] and at_start(s, -COEF):
                        gather_matrix()
                    if pair == at["rstd_back"] and live(s, BACK):
                        rstd_back()
                    if pair == at["rstd_tail"] and live(s, TAIL):
                        rstd_tail()

            steps(step, pool)

        @block.scalar
        def _(act):
            a = nc.scalar
            EXP_LN = "natural_log_exp_and_others"
            act.preload_act_table_set(EXP_LN)
            act.wait_ge(s_consts, 32)
            a.activation(neg_a[:, :], col("Alog"), ACT.Exp).then_inc(s_act, 1)
            act.wait_ge(s_act, 1)
            a.activation(neg_a[:, :], neg_a[:, :], ACT.Copy, scale=-1.0).then_inc(s_act, 1)
            act.wait_ge(s_act, 2)

            def step(s):
                q = s.base % 2
                h_f, h_c, h_b = s + FRONT, s + COEF, s + BACK
                h_h, h_t = s + FFN, s + TAIL
                qf, qc = h_f.base % 2, h_c.base % 2

                def exp_block(m, k):
                    wait(act, s_dps, m.times(BLOCKS, k + 1))
                    wait(act, s_state, m.times(BLOCKS, k + 1 - DECAYS))
                    starts = lambda v: v.rearrange("p (b t) -> p b t", b=NB)[:, :, 1:]
                    a.activation(starts(decay[:, k % DECAYS]), starts(dt_ps[:, :]), ACT.Exp,
                                 scale=neg_a[:, k:k + 1]).then_inc(s_decay, 1)

                def pre_parts():
                    wait(act, s_preps, h_f.times(1, 1))
                    wait(act, s_dt, h_f.times(1, 0))
                    a.activation(relu_pre[:, :], side[0][:, :], ACT.Relu, bias=b_pre[:, 0:1])
                    a.activation(soft_pre[:, :], side[0][:, :], ACT.Abs, bias=b_pre[:, 0:1]).then_inc(s_abs, 1)

                def pre_exp():
                    wait(act, s_abs, h_c.times(1, 1))
                    a.activation(soft_pre[:, :], soft_pre[:, :], ACT.Exp, scale=-1.0).then_inc(s_exp, 1)

                def pre_ln():
                    wait(act, s_exp, h_c.times(1, 1))
                    a.activation(ln_pre[:, :], soft_pre[:, :], ACT.Ln, bias=1.0).then_inc(s_ln, 1)

                def copy_BC():
                    wait(act, s_bcps, h_c.times(1, 1))
                    wait(act, s_b, h_c.times(16, 0))
                    wait(act, s_c, h_c.times(16, 0))
                    a.activation(bc[:, :], side[1][0:2 * NSTATE, :], ACT.Identity,
                                 bias=col("bBC")[0:2 * NSTATE]).then_inc(s_bc, 1)

                def hi_part():
                    wait(act, s_dtx, h_c.times(1, 1))
                    if h_c.i is not None or h_c.base > 0:
                        wait(act, s_stack[1 - qc], (h_c + -1).halves(16 * 12, 16 * 12))
                    a.copy(parts[:, 0], drive_in[:, :, :]).then_inc(s_hi, 1)

                def mid_part():
                    wait(act, s_rest, h_c.times(1, 1))
                    a.copy(parts[:, 1], rest[:, :, :]).then_inc(s_mid, 1)

                def copy_y():
                    wait(act, s_sum, h_b.times(ROUNDS_I, ROUNDS_I))
                    wait(act, s_ytps, h_b.times(1, 0))
                    a.copy(y_sb[:, :], y_ps[:, :]).then_inc(s_y, 1)

                def copy_zT():
                    wait(act, s_ztps, h_f.times(1, 1))
                    wait(act, s_skip, h_f.times(1, -1))
                    wait(act, s_dtx, h_f.times(1, -1))
                    a.copy(zT[:, qf, :, 1:SEQ + 1],
                           side[1][:, :].rearrange("p (b t) -> p b t", b=NB)).then_inc(s_zt, 1)

                def copy_zzT():
                    wait(act, s_zztps, h_h.times(1, 1))
                    wait(act, s_hid, h_h.times(HC, 0))
                    a.copy(zzT[:, :], side[1][:, :]).then_inc(s_zzt, 1)

                def silu():
                    wait(act, s_conv, h_f.times(1, 1))
                    wait(act, s_bcps, h_f.times(1, 0))
                    a.activation(u[:, :], side[1][:, :], ACT.Silu).then_inc(s_u, 1)

                def gelu(c):
                    wait(act, s_hid, h_h.times(HC, c + 1))
                    if c == 0:
                        wait(act, s_sums, h_h.times(1, 0))
                    a.activation(hid[:, c], side[HIDDEN_BANK[c]][:, :], ACT.Gelu,
                                 bias=bias1[:, c:c + 1]).then_inc(s_gelu, 1)

                def square(n):
                    wait(act, s_gelu, h_t.times(HC, 2 * n + 2))
                    a.activation(hid_sq[:, 2 * n:2 * n + 2], hid[:, 2 * n:2 * n + 2],
                                 ACT.Square).then_inc(s_sq, 1)

                def copy_ffnT():
                    wait(act, s_ffntps, h_t.times(1, 1))
                    wait(act, s_ffnps, h_t.times(1, 0))
                    a.copy(ffnT[:, :], side[0][:, :]).then_inc(s_ffnt, 1)

                def copy_sums():
                    wait(act, s_sums, h_t.times(1, 1))
                    wait(act, s_sumst, h_t.times(1, 0))
                    a.copy(sums[:, :], side[1][:, :]).then_inc(s_sumsc, 1)

                at = slots(s, ACT_START, ACT_AT, ACT_END)
                for k in range(BLOCKS):
                    if k == 4 and at_start(s, -FRONT):
                        act.wait_ge(s_dve, SETUP_DIAG)
                    if k == at["pre"] and at_start(s, -FRONT):
                        act.wait_ge(s_dve, SETUP_PRE)
                    if k == 0 and at_start(s, 0):
                        act.wait_ge(s_dve, SETUP_ALL)
                    exps = [(s + b // BLOCKS, b % BLOCKS) for b in DECAY_SLOTS[k]
                            if live(s, b // BLOCKS)]
                    if exps:
                        exp_block(*exps[0])
                    if k == at["exp_pre"] and live(s, COEF):
                        pre_exp()
                    if k == at["zzT"] and live(s, FFN):
                        copy_zzT()
                    if k == at["square0"] and live(s, TAIL):
                        square(0)
                    if exps[1:]:
                        exp_block(*exps[1])
                    if k == at["ln_pre"] and live(s, COEF):
                        pre_ln()
                    if k == at["BC"] and live(s, COEF):
                        copy_BC()
                    if k == at["square1"] and live(s, TAIL):
                        square(1)
                    if k == at["hi"] and live(s, COEF):
                        hi_part()
                    if k == at["y"] and live(s, BACK):
                        copy_y()
                    if k == at["ffnT"] and live(s, TAIL):
                        copy_ffnT()
                    if k == at["sums"] and live(s, TAIL):
                        copy_sums()
                    if k == at["mid"] and live(s, COEF):
                        mid_part()
                    if k == at["zT"] and live(s, FRONT):
                        copy_zT()
                    if k == at["tables"]:
                        if live(s, FRONT):
                            silu()
                        if live(s, FFN):
                            for c in range(HC):
                                gelu(c)
                        if s.i is not None or s.base < LAST:
                            act.preload_act_table_set(EXP_LN)
                    if k == at["pre"] and live(s, FRONT):
                        pre_parts()

            steps(step, act)

        @block.vector
        def _(dve):
            v = nc.vector
            done = [0]

            def link(ins):
                done[0] += 1
                ins.then_inc(s_dve, 1)
                dve.wait_ge(s_dve, done[0])

            v.memset(decay[:, :, :].rearrange("p n (b t) -> p n b t", b=NB)[:, :, :, 0], 0.0)
            v.memset(zT[:, :, :, 0], 0.0)
            link(v.memset(zT[:, :, :, SEQ + 1], 0.0))
            dve.wait_ge(s_consts, 32)
            dve.wait_ge(s_pool, 2)
            for n in range(3):
                link(v.tensor_scalar(diag_conv[:, n], ident[:, :], col("conv")[:, n:n + 1], None, ALU.mult))
            link(v.tensor_scalar(diag_D[:, :], ident[:, :], col("D"), None, ALU.mult))
            assert done[0] == SETUP_DIAG

            w_raw = consts[:, COLS["w1T"][0]:COLS["w1T"][0] + 2 * HID].rearrange("p (a n) -> p a n", a=2)

            def weight_sums():
                dve.wait_ge(s_pe, 1)
                link(v.tensor_copy(w_pre[:, :], y_ps[:, 0:P]))
                link(v.tensor_tensor(b_pre[:, :], y_ps[:, P:P + 1], col("bdtp"), ALU.add))
                assert done[0] == SETUP_PRE
                dve.wait_ge(s_weights, 32)
                link(v.scalar_tensor_tensor(wtmp, w_raw, -1.0, w_raw, ALU.mult, ALU.max))
                link(v.reduce_sum(wsum[:, :], wtmp, AX.X))
                assert done[0] == SETUP_SUMS

            def quantise():
                dve.wait_ge(s_pe, 2)
                link(v.tensor_scalar(wscale[:, 0:2], y_ps[:, 3 * P:3 * P + 2], 1.0 / (HID * P), 1e-5, ALU.mult, ALU.max))
                link(v.reciprocal(wscale[:, 2:4], wscale[:, 0:2]))
                link(v.reciprocal(wscale[:, 0:2], wscale[:, 2:4]))
                for m in range(2):
                    last = v.tensor_scalar(wtmp[:, m], w_raw[:, m], wscale[:, 2 + m:3 + m], 1.0, ALU.mult, ALU.min)
                link(last)
                link(v.tensor_scalar(wq[:, :, :], wtmp, -1.0, RINT, ALU.max, ALU.add))
                link(v.tensor_scalar(wtmp, wq[:, :, :], RINT, None, ALU.subtract))
                for m in range(2):
                    last = v.scalar_tensor_tensor(wq[:, m], wtmp[:, m], wscale[:, m:m + 1], w_raw[:, m],
                                                  ALU.mult, ALU.subtract)
                link(last)
                link(v.tensor_tensor(wq[:, :, :], wq[:, :, :], w_raw, ALU.add))
                link(v.tensor_scalar(w1g[:, :], wq[:, 0], col("g1"), None, ALU.mult))
                for c in range(HC):
                    v.tensor_scalar(w2g[:, c], wq[:, 1, c * P:(c + 1) * P], col("g2")[:, c:c + 1], None, ALU.mult)
                    last = v.tensor_scalar(lb2m[:, c], ones[:, :], col("lb2")[:, c:c + 1], None, ALU.mult)
                link(last)
                assert done[0] == SETUP_GAINS

            def finish_constants():
                dve.wait_ge(s_pe, 3)
                link(v.tensor_tensor(bias1[:, :], y_ps[:, 4:4 + HC], col("b1"), ALU.add))
                link(v.tensor_copy(const_row[:, :], y_ps[:, 2 * P:3 * P]))
                for c in range(HC):
                    last = v.tensor_tensor(w2c[:, c], w2g[:, c], y_ps[:, P:2 * P], ALU.subtract)
                link(last)
                assert done[0] == SETUP_ALL

            def step(s):
                q = s.base % 2
                h_n, h_c, h_b, h_t = s + FRONT, s + COEF, s + BACK, s + TAIL
                qn, qc, qb, qt = (h.base % 2 for h in (h_n, h_c, h_b, h_t))

                def drive_block(m, k):
                    wait(dve, s_xps, m.times(BLOCKS, k + 1))
                    if k == 0:
                        wait(dve, s_b, m.times(16, 16))
                    v.tensor_tensor(driven[drive_bank(k)][:, :], driven[drive_bank(k)][:, :], B_rep[:, m.base % 2],
                                    ALU.mult).then_inc(s_driven, 1)

                def scan_block(k):
                    wait(dve, s_decay, s.times(BLOCKS, k + 1))
                    wait(dve, s_driven, s.times(BLOCKS, k + 1))
                    if k % 2 == 0:
                        wait(dve, s_gated, s.times(PAIRS, k // 2 + 1 - 4))
                    v.tensor_tensor_scan(state[:, (k // 2) % 4, k % 2], decay[:, k % DECAYS],
                                         driven[drive_bank(k)][:, :], 0.0, ALU.mult, ALU.add).then_inc(s_state, 1)

                def moments(n, stats, m, done, h, scale, plus):
                    wait(dve, done, h.times(4, n + 1))
                    if n == 0:
                        v.tensor_tensor(m[:, 0], stats[:, :, 1], stats[:, :, 4], ALU.add)
                        v.tensor_tensor(m[:, 1], stats[:, :, 1], stats[:, :, 4], ALU.subtract)
                        v.tensor_tensor(m[:, 2], stats[:, :, 2], stats[:, :, 5], ALU.add).then_inc(done, 1)
                    elif n == 1:
                        v.tensor_scalar(m[:, 4], m[:, 0], 0.5, None, ALU.mult)
                        v.scalar_tensor_tensor(m[:, 3], m[:, 1], 0.25, m[:, 1], ALU.mult, ALU.mult)
                        v.tensor_scalar(m[:, 5], m[:, 2], scale / P, plus, ALU.mult, ALU.add).then_inc(done, 1)
                    else:
                        v.scalar_tensor_tensor(m[:, 6], m[:, 3], scale, m[:, 5],
                                               ALU.mult, ALU.add).then_inc(done, 1)

                def norm_moments(n):
                    moments(n, stats_f, mom_f, s_fstat, h_n, 1.0, EPS)

                def back_moments(n):
                    moments(n, stats_b, mom_b, s_bstat, h_b, 1.0 + EPS, EPS * EPS)

                def norm_stats():
                    wait(dve, s_xf[qn], h_n.halves(16, 16))
                    for n in range(TT):
                        last = v.bn_stats(stats_f[:, n], xf[:, qn, n])
                    last.then_inc(s_fstat, 1)

                def norm_z():
                    wait(dve, s_frstd, h_n.times(1, 1))
                    wait(dve, s_ztps, h_n.times(1, 0))
                    for n in range(TT):
                        last = v.tensor_scalar(z[:, n], xf[:, qn, n], mom_f[:, 4, n:n + 1], rstd_f[:, n:n + 1],
                                               ALU.subtract, ALU.mult)
                    last.then_inc(s_z, 1)

                def dt_parts():
                    wait(dve, s_rest, h_c.times(1, 0))
                    wait(dve, s_ln, h_c.times(1, 1))
                    wait(dve, s_zt, h_c.times(1, 1))
                    v.tensor_tensor(drive_in[:, 0], relu_pre[:, :], ln_pre[:, :], ALU.add).then_inc(s_dt, 1)
                    wait(dve, s_dt, h_c.times(1, 1))
                    v.tensor_tensor(drive_in[:, 1].rearrange("p (b t) -> p b t", b=NB),
                                    drive_in[:, 0].rearrange("p (b t) -> p b t", b=NB),
                                    zT[:, qc, :, 1:SEQ + 1], ALU.mult).then_inc(s_dtx, 1)

                def back_residual():
                    wait(dve, s_ytps, h_b.times(1, 1))
                    wait(dve, s_xb, h_b.times(16, 16))
                    wait(dve, s_x2c, h_b.times(1, -1))
                    v.tensor_tensor(x2[:, qb], xb[:, :, :],
                                    side[2][:, :].rearrange("p (n d) -> p n d", n=TT),
                                    ALU.add).then_inc(s_x2, 1)
                    wait(dve, s_x2, h_b.times(1, 1))
                    for n in range(TT):
                        last = v.bn_stats(stats_b[:, n], x2[:, qb, n])
                    last.then_inc(s_bstat, 1)

                def back_zz():
                    wait(dve, s_brstd, h_b.times(1, 1))
                    wait(dve, s_zztps, h_b.times(1, 0))
                    for n in range(TT):
                        last = v.tensor_scalar(zz[:, n], x2[:, qb, n], mom_b[:, 4, n:n + 1], rstd_b[:, n:n + 1],
                                               ALU.subtract, ALU.mult)
                    last.then_inc(s_zz, 1)

                def tail_stats(n):
                    if n > 0:
                        wait(dve, s_tstat, h_t.times(4, n))
                    if n == 0:
                        groups = side[0][:, :].rearrange("p (n c w r) -> p w n c r",
                                                         n=TT, c=HC, w=2)[:, :, :, :, 0]
                        wait(dve, s_sumst, h_t.times(1, 1))
                        ins = v.reduce_sum(mom_t[:, 0:2], groups, AX.X)
                    elif n == 1:
                        ins = v.scalar_tensor_tensor(mom_t[:, 2], mom_t[:, 0], 1.0 / HID ** 2, mom_t[:, 0],
                                                     ALU.mult, ALU.mult)
                    elif n == 2:
                        ins = v.scalar_tensor_tensor(mom_t[:, 3], mom_t[:, 1], 1.0 / HID, mom_t[:, 2],
                                                     ALU.mult, ALU.subtract)
                    else:
                        ins = v.tensor_scalar(mom_t[:, 4], mom_t[:, 3], 0.0, EPS, ALU.max, ALU.add)
                    ins.then_inc(s_tstat, 1)

                def tail_result():
                    wait(dve, s_x2c, h_t.times(1, 1))
                    wait(dve, s_out[qt], h_t.halves(16, 16))
                    wait(dve, s_ffnps, h_t.times(1, 1))
                    wait(dve, s_trstd, h_t.times(1, 1))
                    for n in range(TT):
                        last = v.scalar_tensor_tensor(ob[:, qt, n], side[2][:, n * P:(n + 1) * P],
                                                      rstd_t[:, n:n + 1], x2c[:, n], ALU.mult, ALU.add)
                    last.then_inc(s_res, 1)

                if s.i is None and s.base == 0:
                    drive_block(s, 0)
                at = slots(s, DVE_START, DVE_AT, DVE_END)
                def between(place):
                    for n in range(3):
                        if place == 2 * at["norm_stats"] + 2 + n and live(s, FRONT):
                            norm_moments(n)
                        if place == 2 * at["residual"] + 2 + n and live(s, BACK):
                            back_moments(n)
                        if place == 2 * at["tail_stats"] + 2 + n and live(s, TAIL):
                            tail_stats(n + 1)

                for k in range(BLOCKS):
                    if live(s, SCAN):
                        if k < BLOCKS - 1:
                            drive_block(s, k + 1)
                    between(2 * k)
                    if live(s, SCAN):
                        scan_block(k)
                    between(2 * k + 1)
                    if k == BLOCKS - 1 and live(s, SCAN) and live(s + 1, SCAN):
                        drive_block(s + 1, 0)
                    if k == at["norm_stats"] and live(s, FRONT):
                        norm_stats()
                    if k == at["norm_stats"] + 2 and at_start(s, -FRONT):
                        weight_sums()
                    if k == at["norm_z"] + 1 and at_start(s, -FRONT):
                        quantise()
                    if k == 6 and at_start(s, 1 - FRONT):
                        finish_constants()
                    if k == at["dt_parts"] and live(s, COEF):
                        dt_parts()
                    if k == at["norm_z"] and live(s, FRONT):
                        norm_z()
                    if k == at["residual"] and live(s, BACK):
                        back_residual()
                    if k == at["tail_stats"] and live(s, TAIL):
                        tail_stats(0)
                    if k == at["zz"] and live(s, BACK):
                        back_zz()
                    if k == at["result"] and live(s, TAIL):
                        tail_result()

            steps(step, dve)

        @block.tensor
        def _(pe):
            mm = nc.tensor.matmul
            pe.wait_ge(s_consts, 32)
            mm(y_ps[:, 0:P], dtw[:, 0:P], dtw[:, P:2 * P], start=True, stop=True)
            mm(y_ps[:, P:P + 1], dtw[:, P:2 * P], dtw[:, 2 * P:2 * P + 1], start=True, stop=True).then_inc(s_pe, 1)
            pe.wait_ge(s_pool, 2)
            pe.wait_ge(s_dve, SETUP_DIAG)

            def weight_totals():
                pe.wait_ge(s_dve, SETUP_SUMS)
                mm(y_ps[:, 3 * P:3 * P + 2], ones[:, :], wsum[:, :], start=True, stop=True).then_inc(s_pe, 1)

            def constant_products():
                pe.wait_ge(s_dve, SETUP_GAINS)
                for c in range(HC):
                    mm(y_ps[:, 4 + c:5 + c], wq[:, 0, c * P:(c + 1) * P], col("lb1"), start=True, stop=True)
                for c in range(HC):
                    mm(y_ps[:, P:2 * P], avg[:, :], w2g[:, c], start=(c == 0), stop=(c == HC - 1))
                for c in range(HC):
                    mm(y_ps[:, 2 * P:3 * P], lb2m[:, c], wq[:, 1, c * P:(c + 1) * P], start=(c == 0), stop=False)
                mm(y_ps[:, 2 * P:3 * P], ones[0:1, :], b2r[:, :], start=False, stop=True).then_inc(s_pe, 1)

            def step(s):
                q = s.base % 2
                h_f, h_c, h_b = s + FRONT, s + COEF, s + BACK
                h_h, h_t = s + FFN, s + TAIL

                def spread_dt(m, k):
                    if k == 0:
                        wait(pe, s_stack[m.base % 2], m.halves(16 * 12, 16 * 12))
                    wait(pe, s_decay, m.times(BLOCKS, k))
                    mm(dt_ps[:, :], spread[0:96, k // QUAD], stacked[0:96, m.base % 2, k % QUAD, 0],
                       start=True, stop=True).then_inc(s_dps, 1)

                def spread_dtx(k):
                    wait(pe, s_state, s.times(BLOCKS, k + 1 - drive_before(k)))
                    mm(driven[drive_bank(k)][:, :], spread[0:96, k // QUAD], stacked[0:96, q, k % QUAD, 1],
                       start=True, stop=True).then_inc(s_xps, 1)

                def sum_quad(m, i):
                    wait(pe, s_gated, m.times(PAIRS, 2 * i + 2))
                    for j in range(QUAD):
                        last = mm(y_ps[32 * j:32 * j + 32, :], gather[:, i], gated[:, i, j],
                                  start=False, stop=(i == ROUNDS_I - 1), skip_group_check=True)
                    last.then_inc(s_sum, 1)

                def skip_term():
                    wait(pe, s_y, s.times(1, 0))
                    mm(y_ps[:, :].rearrange("p (b t) -> p b t", b=NB), diag_D[:, :], zT[:, q, :, 1:SEQ + 1],
                       start=True, stop=False, skip_group_check=True).then_inc(s_skip, 1)

                def bank_read(*readers):
                    for stage, read, per, count in readers:
                        if live(s, stage):
                            wait(pe, read, (s + stage).times(per, count))
                            return

                def transposes(to, source, done):
                    for n in range(TT):
                        last = nc.tensor.transpose(side[to][:, n * P:(n + 1) * P], source(n), ident[:, :])
                    last.then_inc(done, 1)

                def convolve(n):
                    if n == 0:
                        wait(pe, s_zt, h_f.times(1, 1))
                    ins = mm(side[1][:, :].rearrange("p (b t) -> p b t", b=NB), diag_conv[:, n],
                             zT[:, h_f.base % 2, :, n:n + SEQ], start=(n == 0), stop=(n == 2))
                    if n == 2:
                        ins.then_inc(s_conv, 1)

                def first(c):
                    if c == 0:
                        wait(pe, s_zzt, h_h.times(1, 1))
                        bank_read((BACK, s_x2, 1, 1),
                                  (TAIL - 1, s_res, 1, 1))
                    elif c == 1:
                        bank_read((TAIL, s_tstat, 4, 1),
                                  (FRONT - 1, s_abs, 1, 1))
                    elif c == 2:
                        bank_read((FRONT, s_u, 1, 1),
                                  (TAIL, s_sumsc, 1, 1),
                                  (COEF, s_bc, 1, 1))
                    else:
                        wait(pe, s_gelu, h_h.times(HC, 1))
                    mm(side[HIDDEN_BANK[c]][:, :], w1g[:, c * P:(c + 1) * P], zzT[:, :],
                       start=True, stop=True).then_inc(s_hid, 1)

                def pre():
                    wait(pe, s_u, h_f.times(1, 1))
                    bank_read((FFN, s_gelu, HC, 2),
                              (FRONT - 1, s_abs, 1, 1))
                    mm(side[0][:, :], w_pre[:, :], u[:, :], start=True, stop=True).then_inc(s_preps, 1)

                def fill_BC():
                    wait(pe, s_u, h_c.times(1, 1))
                    bank_read((BACK - 1, s_zzt, 1, 1))
                    mm(side[1][0:2 * NSTATE, :], col("wBC"), u[:, :], start=True, stop=True).then_inc(s_bcps, 1)

                def second(c):
                    if c == 0:
                        wait(pe, s_gelu, h_t.times(HC, HC))
                        bank_read((FRONT - 1, s_abs, 1, 1))
                    ins = mm(side[0][:, :], w2c[:, c], hid[:, c], start=(c == 0), stop=(c == HC - 1))
                    if c == HC - 1:
                        ins.then_inc(s_ffntps, 1)

                def hidden_sums(n):
                    if n == 0:
                        bank_read((COEF, s_bc, 1, 1),
                                  (BACK - 1, s_zzt, 1, 1))
                    else:
                        wait(pe, s_sq, h_t.times(2, 2))
                    for c in range(HC):
                        last = mm(side[1][32 * c:32 * c + 32, :], pick_sum[:, n], (hid, hid_sq)[n][:, c],
                                  start=(n == 0), stop=(n == 1), skip_group_check=True)
                    if n == 1:
                        last.then_inc(s_sums, 1)

                def transpose_y():
                    wait(pe, s_y, h_b.times(1, 1))
                    bank_read((TAIL - 1, s_res, 1, 1),
                              (FFN - 1, s_gelu, HC, HC),
                              (BACK - 1, s_x2, 1, 1))
                    transposes(2, lambda n: y_sb[:, n * P:(n + 1) * P], s_ytps)

                def transpose_sums():
                    wait(pe, s_sumsc, h_t.times(1, 1))
                    wait(pe, s_ffnt, h_t.times(1, 1))
                    transposes(0, lambda n: sums[:, n * P:(n + 1) * P], s_sumst)

                def transpose_z():
                    wait(pe, s_z, h_f.times(1, 1))
                    bank_read((TAIL, s_sumsc, 1, 1),
                              (COEF, s_bc, 1, 1))
                    transposes(1, lambda n: z[:, n], s_ztps)

                def transpose_zz():
                    wait(pe, s_zz, h_b.times(1, 1))
                    bank_read((FFN, s_gelu, HC, 3),
                              (FRONT, s_u, 1, 1),
                              (TAIL, s_sumsc, 1, 1),
                              (COEF, s_bc, 1, 1))
                    transposes(1, lambda n: zz[:, n], s_zztps)

                def transpose_ffn():
                    wait(pe, s_ffnt, h_t.times(1, 1))
                    bank_read((FFN, s_gelu, HC, HC),
                              (BACK, s_x2, 1, 1),
                              (TAIL - 1, s_res, 1, 1))
                    transposes(2, lambda n: ffnT[:, n * P:(n + 1) * P], s_ffnps)

                at = slots(s, PE_START, PE_AT, PE_END)
                for k in range(BLOCKS):
                    second_dt = [b for b in DECAY_SLOTS[k][1:] if live(s, b // BLOCKS)]
                    next_dt = [b + BLOCKS * ((k + 1) // BLOCKS) for b in DECAY_SLOTS[(k + 1) % BLOCKS][:1]]
                    next_dt = [b for b in next_dt if live(s, b // BLOCKS)]
                    if k == 7 and at_start(s, -FRONT):
                        weight_totals()
                    if k == at["pre"] and at_start(s, -FRONT):
                        pe.wait_ge(s_dve, SETUP_PRE)
                    if k == 7 and at_start(s, 1 - FRONT):
                        constant_products()
                    if k == BLOCKS + DECAY_AT[0] - 1 and at_start(s, 1 - FRONT):
                        pe.wait_ge(s_pool, 2 + PARTS)
                    if k == 0 and at_start(s, 0):
                        pe.wait_ge(s_dve, SETUP_ALL)
                    if k == at["quad0"] and at_start(s, 0):
                        pe.wait_ge(s_pool, 2 + PARTS + NSTATE)
                    if live(s, SCAN):
                        spread_dtx(k)
                    for c in range(HC):
                        if k == at["second"][c] and live(s, TAIL):
                            second(c)
                    if k == at["skip"] and live(s, SCAN):
                        skip_term()
                    for b in second_dt:
                        spread_dt(s + b // BLOCKS, b % BLOCKS)
                    if k == at["quad2"] and live(s, BACK):
                        sum_quad(h_b, 2)
                    if k == at["BC"] and live(s, COEF):
                        fill_BC()
                    if k == at["quad3"] and live(s, BACK):
                        sum_quad(h_b, 3)
                    for n in range(2):
                        if k == at["sums"][n] and live(s, TAIL):
                            hidden_sums(n)
                    if k == at["yT"] and live(s, BACK):
                        transpose_y()
                    if k == at["zT"] and live(s, FRONT):
                        transpose_z()
                    if k == at["quad0"] and live(s, SCAN):
                        sum_quad(s, 0)
                    if k == at["sumsT"] and live(s, TAIL):
                        transpose_sums()
                    for n in range(3):
                        if k == at["conv"][n] and live(s, FRONT):
                            convolve(n)
                    for c in range(HC):
                        if k == at["first"][c] and live(s, FFN):
                            first(c)
                    if k == at["quad1"] and live(s, SCAN):
                        sum_quad(s, 1)
                    if k == at["pre"] and live(s, FRONT):
                        pre()
                    if k == at["zzT"] and live(s, BACK):
                        transpose_zz()
                    if k == at["ffn"] and live(s, TAIL):
                        transpose_ffn()
                    for b in next_dt:
                        spread_dt(s + b // BLOCKS, b % BLOCKS)

            steps(step, pe)


def kernel(**inputs):
    import numpy as np
    import concourse.bacc as bacc
    from concourse.bass_utils import run_bass_kernel_spmd

    a = {k: np.asarray(v) for k, v in inputs.items()}
    f = lambda name: a["L0_" + name]
    xs = f("attn_x")
    tokens = xs.shape[0] * xs.shape[1]
    a_log = f("attn_A_log").reshape(QUAD, ROUNDS_I, DSUB, NSTATE).transpose(3, 2, 1, 0).reshape(P, BLOCKS)
    w_bc, b_bc = f("attn_W_bc"), f("attn_b_bc")
    packed = {
        "conv": f("attn_conv_w").T,
        "bBC": np.concatenate([b_bc, np.zeros(P - 2 * NSTATE, b_bc.dtype)])[:, None],
        "bdtp": f("attn_b_dtp")[:, None], "D": f("attn_Dcoeff")[:, None],
        "g1": f("ffn_ln1_g")[:, None], "lb1": f("ffn_ln1_b")[:, None],
        "b1": f("ffn_b1").reshape(HC, P).T, "g2": f("ffn_ln2_g").reshape(HC, P).T,
        "lb2": f("ffn_ln2_b").reshape(HC, P).T, "Alog": a_log,
        "wBC": w_bc,
        "w1T": f("ffn_w1").T,
        "w2T": f("ffn_w2").T.reshape(HC, P, P).transpose(1, 0, 2).reshape(P, HID),
    }
    arrays = {
        "x": np.ascontiguousarray(xs.reshape(tokens, P)),
        "cols": np.ascontiguousarray(np.concatenate([packed[k] for k in COLS], axis=1)),
        "dt_rows": np.ascontiguousarray(np.concatenate(
            [f("attn_W_dt").T, f("attn_W_dtp"), f("attn_b_dt")[:, None]], axis=1)),
        "b2_row": np.ascontiguousarray(f("ffn_b2")[None, :]),
    }
    nc = bacc.Bacc("TRN2", target_bir_lowering=False, num_devices=1)
    aps = [nc.dram_tensor(k, v.shape, mybir.dt.from_np(v.dtype), kind="ExternalInput").ap()
           for k, v in arrays.items()]
    out = nc.dram_tensor("out", (tokens, P), F32, kind="ExternalOutput").ap()
    preln_ssm_ffn(nc, *aps, out, tokens // CHUNK)
    r = run_bass_kernel_spmd(nc, [arrays], core_ids=[0])
    return r.results[0]["out"].reshape(xs.shape)
```
